# Optimizing a Trainium2 kernel written in Bass

```python
import numpy as np
import jax
import jax.numpy as jnp

def _softmax(x, axis=-1):
    return jax.nn.softmax(x, axis=axis)

def _gelu(x):
    return jax.nn.gelu(x, approximate=True)

def _silu(x):
    return jax.nn.silu(x)

def _sigmoid(x):
    return jax.nn.sigmoid(x)

def _layernorm(x, axis=-1, eps=1e-05):
    m = jnp.mean(x, axis=axis, keepdims=True)
    v = jnp.var(x, axis=axis, keepdims=True)
    return (x - m) / jnp.sqrt(v + eps)

def _scatter_add(tgt, idx, src, axis=0):
    return tgt.at[idx].add(src)

def _segment_sum(src, seg, n):
    return jax.ops.segment_sum(src, seg, n)
kernel_name = 'mk_rec_standalone_d1_rec_r8_9031f2'

def setup_inputs(seed: int=0):
    np.random.seed(seed)
    _w = jnp.asarray

    def _rec_inputs():
        import jax
        import jax.numpy as jnp
        _rk = jax.random.key(seed)
        r_items = jnp.stack([jax.random.randint(jax.random.fold_in(jax.random.fold_in(_rk, 1), 0), (512,), 76, 99919, jnp.int32), jax.random.randint(jax.random.fold_in(jax.random.fold_in(_rk, 1), 1), (512,), 55, 99454, jnp.int32), jax.random.randint(jax.random.fold_in(jax.random.fold_in(_rk, 1), 2), (512,), 29, 99986, jnp.int32), jax.random.randint(jax.random.fold_in(jax.random.fold_in(_rk, 1), 3), (512,), 67, 99935, jnp.int32), jax.random.randint(jax.random.fold_in(jax.random.fold_in(_rk, 1), 4), (512,), 209, 99887, jnp.int32), jax.random.randint(jax.random.fold_in(jax.random.fold_in(_rk, 1), 5), (512,), 176, 99942, jnp.int32), jax.random.randint(jax.random.fold_in(jax.random.fold_in(_rk, 1), 6), (512,), 1, 99939, jnp.int32), jax.random.randint(jax.random.fold_in(jax.random.fold_in(_rk, 1), 7), (512,), 31, 99945, jnp.int32), jax.random.randint(jax.random.fold_in(jax.random.fold_in(_rk, 1), 8), (512,), 95, 99951, jnp.int32), jax.random.randint(jax.random.fold_in(jax.random.fold_in(_rk, 1), 9), (512,), 13, 12482, jnp.int32), jax.random.randint(jax.random.fold_in(jax.random.fold_in(_rk, 1), 10), (512,), 70, 99701, jnp.int32), jax.random.randint(jax.random.fold_in(jax.random.fold_in(_rk, 1), 11), (512,), 146, 99964, jnp.int32), jax.random.randint(jax.random.fold_in(jax.random.fold_in(_rk, 1), 12), (512,), 39, 12467, jnp.int32), jax.random.randint(jax.random.fold_in(jax.random.fold_in(_rk, 1), 13), (512,), 6, 99887, jnp.int32), jax.random.randint(jax.random.fold_in(jax.random.fold_in(_rk, 1), 14), (512,), 323, 99835, jnp.int32), jax.random.randint(jax.random.fold_in(jax.random.fold_in(_rk, 1), 15), (512,), 131, 99917, jnp.int32), jax.random.randint(jax.random.fold_in(jax.random.fold_in(_rk, 1), 16), (512,), 28, 99865, jnp.int32), jax.random.randint(jax.random.fold_in(jax.random.fold_in(_rk, 1), 17), (512,), 20, 99962, jnp.int32), jax.random.randint(jax.random.fold_in(jax.random.fold_in(_rk, 1), 18), (512,), 86, 99873, jnp.int32), jax.random.randint(jax.random.fold_in(jax.random.fold_in(_rk, 1), 19), (512,), 18, 12488, jnp.int32), jax.random.randint(jax.random.fold_in(jax.random.fold_in(_rk, 1), 20), (512,), 17, 99987, jnp.int32), jax.random.randint(jax.random.fold_in(jax.random.fold_in(_rk, 1), 21), (512,), 231, 99946, jnp.int32), jax.random.randint(jax.random.fold_in(jax.random.fold_in(_rk, 1), 22), (512,), 264, 99913, jnp.int32), jax.random.randint(jax.random.fold_in(jax.random.fold_in(_rk, 1), 23), (512,), 32, 99861, jnp.int32), jax.random.randint(jax.random.fold_in(jax.random.fold_in(_rk, 1), 24), (512,), 78, 99953, jnp.int32), jax.random.randint(jax.random.fold_in(jax.random.fold_in(_rk, 1), 25), (512,), 90, 12459, jnp.int32), jax.random.randint(jax.random.fold_in(jax.random.fold_in(_rk, 1), 26), (512,), 98, 99911, jnp.int32), jax.random.randint(jax.random.fold_in(jax.random.fold_in(_rk, 1), 27), (512,), 104, 99805, jnp.int32), jax.random.randint(jax.random.fold_in(jax.random.fold_in(_rk, 1), 28), (512,), 71, 99870, jnp.int32), jax.random.randint(jax.random.fold_in(jax.random.fold_in(_rk, 1), 29), (512,), 185, 99594, jnp.int32), jax.random.randint(jax.random.fold_in(jax.random.fold_in(_rk, 1), 30), (512,), 394, 99938, jnp.int32), jax.random.randint(jax.random.fold_in(jax.random.fold_in(_rk, 1), 31), (512,), 116, 99794, jnp.int32), jax.random.randint(jax.random.fold_in(jax.random.fold_in(_rk, 1), 32), (512,), 100, 99954, jnp.int32), jax.random.randint(jax.random.fold_in(jax.random.fold_in(_rk, 1), 33), (512,), 17, 99946, jnp.int32), jax.random.randint(jax.random.fold_in(jax.random.fold_in(_rk, 1), 34), (512,), 46, 99945, jnp.int32), jax.random.randint(jax.random.fold_in(jax.random.fold_in(_rk, 1), 35), (512,), 19, 99949, jnp.int32), jax.random.randint(jax.random.fold_in(jax.random.fold_in(_rk, 1), 36), (512,), 148, 99807, jnp.int32), jax.random.randint(jax.random.fold_in(jax.random.fold_in(_rk, 1), 37), (512,), 64, 99906, jnp.int32), jax.random.randint(jax.random.fold_in(jax.random.fold_in(_rk, 1), 38), (512,), 53, 99948, jnp.int32), jax.random.randint(jax.random.fold_in(jax.random.fold_in(_rk, 1), 39), (512,), 14, 99978, jnp.int32), jax.random.randint(jax.random.fold_in(jax.random.fold_in(_rk, 1), 40), (512,), 88, 99969, jnp.int32), jax.random.randint(jax.random.fold_in(jax.random.fold_in(_rk, 1), 41), (512,), 1, 99884, jnp.int32), jax.random.randint(jax.random.fold_in(jax.random.fold_in(_rk, 1), 42), (512,), 79, 99847, jnp.int32), jax.random.randint(jax.random.fold_in(jax.random.fold_in(_rk, 1), 43), (512,), 45, 99942, jnp.int32), jax.random.randint(jax.random.fold_in(jax.random.fold_in(_rk, 1), 44), (512,), 5, 12484, jnp.int32), jax.random.randint(jax.random.fold_in(jax.random.fold_in(_rk, 1), 45), (512,), 213, 99855, jnp.int32), jax.random.randint(jax.random.fold_in(jax.random.fold_in(_rk, 1), 46), (512,), 142, 99809, jnp.int32), jax.random.randint(jax.random.fold_in(jax.random.fold_in(_rk, 1), 47), (512,), 62, 99821, jnp.int32), jax.random.randint(jax.random.fold_in(jax.random.fold_in(_rk, 1), 48), (512,), 3, 99964, jnp.int32), jax.random.randint(jax.random.fold_in(jax.random.fold_in(_rk, 1), 49), (512,), 82, 99919, jnp.int32)], axis=1)
        r_inputs = jnp.stack([jax.random.randint(jax.random.fold_in(jax.random.fold_in(_rk, 2), 0), (512,), 55, 99965, jnp.int32), jax.random.randint(jax.random.fold_in(jax.random.fold_in(_rk, 2), 1), (512,), 48, 12493, jnp.int32), jax.random.randint(jax.random.fold_in(jax.random.fold_in(_rk, 2), 2), (512,), 149, 99818, jnp.int32), jax.random.randint(jax.random.fold_in(jax.random.fold_in(_rk, 2), 3), (512,), 64, 99943, jnp.int32), jax.random.randint(jax.random.fold_in(jax.random.fold_in(_rk, 2), 4), (512,), 83, 99948, jnp.int32), jax.random.randint(jax.random.fold_in(jax.random.fold_in(_rk, 2), 5), (512,), 54, 99999, jnp.int32), jax.random.randint(jax.random.fold_in(jax.random.fold_in(_rk, 2), 6), (512,), 215, 99939, jnp.int32), jax.random.randint(jax.random.fold_in(jax.random.fold_in(_rk, 2), 7), (512,), 95, 99911, jnp.int32), jax.random.randint(jax.random.fold_in(jax.random.fold_in(_rk, 2), 8), (512,), 33, 99809, jnp.int32), jax.random.randint(jax.random.fold_in(jax.random.fold_in(_rk, 2), 9), (512,), 67, 99845, jnp.int32), jax.random.randint(jax.random.fold_in(jax.random.fold_in(_rk, 2), 10), (512,), 35, 99948, jnp.int32), jax.random.randint(jax.random.fold_in(jax.random.fold_in(_rk, 2), 11), (512,), 56, 99973, jnp.int32), jax.random.randint(jax.random.fold_in(jax.random.fold_in(_rk, 2), 12), (512,), 30, 99941, jnp.int32), jax.random.randint(jax.random.fold_in(jax.random.fold_in(_rk, 2), 13), (512,), 97, 99859, jnp.int32), jax.random.randint(jax.random.fold_in(jax.random.fold_in(_rk, 2), 14), (512,), 23, 99998, jnp.int32), jax.random.randint(jax.random.fold_in(jax.random.fold_in(_rk, 2), 15), (512,), 116, 99994, jnp.int32), jax.random.randint(jax.random.fold_in(jax.random.fold_in(_rk, 2), 16), (512,), 148, 12495, jnp.int32), jax.random.randint(jax.random.fold_in(jax.random.fold_in(_rk, 2), 17), (512,), 206, 99747, jnp.int32), jax.random.randint(jax.random.fold_in(jax.random.fold_in(_rk, 2), 18), (512,), 37, 99628, jnp.int32), jax.random.randint(jax.random.fold_in(jax.random.fold_in(_rk, 2), 19), (512,), 324, 12483, jnp.int32), jax.random.randint(jax.random.fold_in(jax.random.fold_in(_rk, 2), 20), (512,), 89, 12495, jnp.int32), jax.random.randint(jax.random.fold_in(jax.random.fold_in(_rk, 2), 21), (512,), 68, 99881, jnp.int32), jax.random.randint(jax.random.fold_in(jax.random.fold_in(_rk, 2), 22), (512,), 2, 99711, jnp.int32), jax.random.randint(jax.random.fold_in(jax.random.fold_in(_rk, 2), 23), (512,), 311, 99742, jnp.int32), jax.random.randint(jax.random.fold_in(jax.random.fold_in(_rk, 2), 24), (512,), 53, 99950, jnp.int32), jax.random.randint(jax.random.fold_in(jax.random.fold_in(_rk, 2), 25), (512,), 190, 99982, jnp.int32), jax.random.randint(jax.random.fold_in(jax.random.fold_in(_rk, 2), 26), (512,), 216, 99910, jnp.int32), jax.random.randint(jax.random.fold_in(jax.random.fold_in(_rk, 2), 27), (512,), 148, 99953, jnp.int32), jax.random.randint(jax.random.fold_in(jax.random.fold_in(_rk, 2), 28), (512,), 137, 99935, jnp.int32), jax.random.randint(jax.random.fold_in(jax.random.fold_in(_rk, 2), 29), (512,), 122, 12485, jnp.int32), jax.random.randint(jax.random.fold_in(jax.random.fold_in(_rk, 2), 30), (512,), 8, 99927, jnp.int32), jax.random.randint(jax.random.fold_in(jax.random.fold_in(_rk, 2), 31), (512,), 13, 99979, jnp.int32), jax.random.randint(jax.random.fold_in(jax.random.fold_in(_rk, 2), 32), (512,), 120, 99930, jnp.int32), jax.random.randint(jax.random.fold_in(jax.random.fold_in(_rk, 2), 33), (512,), 49, 99972, jnp.int32), jax.random.randint(jax.random.fold_in(jax.random.fold_in(_rk, 2), 34), (512,), 134, 99879, jnp.int32), jax.random.randint(jax.random.fold_in(jax.random.fold_in(_rk, 2), 35), (512,), 12, 99958, jnp.int32), jax.random.randint(jax.random.fold_in(jax.random.fold_in(_rk, 2), 36), (512,), 168, 12497, jnp.int32), jax.random.randint(jax.random.fold_in(jax.random.fold_in(_rk, 2), 37), (512,), 57, 99894, jnp.int32), jax.random.randint(jax.random.fold_in(jax.random.fold_in(_rk, 2), 38), (512,), 231, 99987, jnp.int32), jax.random.randint(jax.random.fold_in(jax.random.fold_in(_rk, 2), 39), (512,), 35, 99956, jnp.int32), jax.random.randint(jax.random.fold_in(jax.random.fold_in(_rk, 2), 40), (512,), 23, 12490, jnp.int32), jax.random.randint(jax.random.fold_in(jax.random.fold_in(_rk, 2), 41), (512,), 114, 99951, jnp.int32), jax.random.randint(jax.random.fold_in(jax.random.fold_in(_rk, 2), 42), (512,), 0, 99894, jnp.int32), jax.random.randint(jax.random.fold_in(jax.random.fold_in(_rk, 2), 43), (512,), 158, 99699, jnp.int32), jax.random.randint(jax.random.fold_in(jax.random.fold_in(_rk, 2), 44), (512,), 28, 99839, jnp.int32), jax.random.randint(jax.random.fold_in(jax.random.fold_in(_rk, 2), 45), (512,), 5, 99956, jnp.int32), jax.random.randint(jax.random.fold_in(jax.random.fold_in(_rk, 2), 46), (512,), 69, 99986, jnp.int32), jax.random.randint(jax.random.fold_in(jax.random.fold_in(_rk, 2), 47), (512,), 4, 99981, jnp.int32), jax.random.randint(jax.random.fold_in(jax.random.fold_in(_rk, 2), 48), (512,), 55, 99931, jnp.int32), jax.random.randint(jax.random.fold_in(jax.random.fold_in(_rk, 2), 49), (512,), 82, 99978, jnp.int32)], axis=1)
        r_alias_inputs = jax.random.randint(jax.random.fold_in(_rk, 3), (512, 50), 0, 50, jnp.int32)
        return (r_items, r_inputs, r_alias_inputs)
    r_items, r_inputs, r_alias_inputs = _rec_inputs()

    def _L0_rec_setup():
        import jax, jax.numpy as jnp
        import numpy as np
        N = 12500
        D = 128
        B = 1024
        L = 50
        NNZ = 200000
        LAYERS = 2
        W_K = 12.0
        EPS = 1e-12

        def _l2norm(x):
            n = jnp.sqrt(jnp.sum(x * x, axis=-1, keepdims=True))
            return x / jnp.maximum(n, EPS)
        key = jax.random.key(seed)
        ks = jax.random.split(key, 12)
        stdv = 1.0 / np.sqrt(D)
        u = lambda k, shape: jax.random.uniform(k, shape, jnp.float32, -stdv, stdv)
        inp = {'items': jax.random.randint(ks[0], (B, L), 0, N), 'inputs': jax.random.randint(ks[1], (B, L), 0, N), 'alias_inputs': jax.random.randint(ks[2], (B, L), 0, L), 'adj_row': jnp.sort(jax.random.randint(ks[3], (NNZ,), 0, N)), 'adj_col': jax.random.randint(ks[4], (NNZ,), 0, N), 'adj_val': jax.random.uniform(ks[5], (NNZ,), jnp.float32), 'E': u(ks[6], (N, D)), 'pos_emb': u(ks[7], (L, D)), 'w1': u(ks[8], (2 * D, D)), 'w2': u(ks[9], (D, 1)), 'glu1_w': u(ks[10], (D, D)), 'glu1_b': jnp.zeros((D,), jnp.float32), 'glu2_w': u(ks[11], (D, D))}
        return inp
    _L0_rec_all = _L0_rec_setup()
    _L0_rec_in = {k: v for k, v in _L0_rec_all.items() if k in ('adj_row', 'adj_col', 'adj_val', 'E', 'pos_emb', 'w1', 'w2', 'glu1_w', 'glu1_b', 'glu2_w')}
    del _L0_rec_all
    return {'r_items': r_items, 'r_inputs': r_inputs, 'r_alias_inputs': r_alias_inputs, 'L0_rec_adj_row': _L0_rec_in['adj_row'], 'L0_rec_adj_col': _L0_rec_in['adj_col'], 'L0_rec_adj_val': _L0_rec_in['adj_val'], 'L0_rec_E': _L0_rec_in['E'], 'L0_rec_pos_emb': _L0_rec_in['pos_emb'], 'L0_rec_w1': _L0_rec_in['w1'], 'L0_rec_w2': _L0_rec_in['w2'], 'L0_rec_glu1_w': _L0_rec_in['glu1_w'], 'L0_rec_glu1_b': _L0_rec_in['glu1_b'], 'L0_rec_glu2_w': _L0_rec_in['glu2_w']}

def reference(r_items, r_inputs, r_alias_inputs, L0_rec_adj_row, L0_rec_adj_col, L0_rec_adj_val, L0_rec_E, L0_rec_pos_emb, L0_rec_w1, L0_rec_w2, L0_rec_glu1_w, L0_rec_glu1_b, L0_rec_glu2_w):
    import jax
    import jax.numpy as jnp

    def _L0_rec_ref(items, inputs, alias_inputs, adj_row, adj_col, adj_val, E, pos_emb, w1, w2, glu1_w, glu1_b, glu2_w):
        import jax, jax.numpy as jnp
        import numpy as np
        N = 12500
        D = 128
        B = 1024
        L = 50
        NNZ = 200000
        LAYERS = 2
        W_K = 12.0
        EPS = 1e-12

        def _l2norm(x):
            n = jnp.sqrt(jnp.sum(x * x, axis=-1, keepdims=True))
            return x / jnp.maximum(n, EPS)

        def spmm(h):
            return jax.ops.segment_sum(adj_val[:, None] * h[adj_col], adj_row, num_segments=N)
        h = E
        acc = E
        for _ in range(LAYERS):
            h = _l2norm(spmm(h))
            acc = acc + h
        graph_item_embs = acc / (LAYERS + 1)
        hidden = graph_item_embs[items]
        seq_hidden = jnp.take_along_axis(hidden, alias_inputs[..., None], axis=1)
        mask = (inputs != 0).astype(seq_hidden.dtype)[..., None]
        hs = jnp.sum(seq_hidden * mask, axis=1) / jnp.sum(mask, axis=1)
        pos = jnp.flip(pos_emb, axis=0)
        pos_b = jnp.broadcast_to(pos[None], (seq_hidden.shape[0], L, D))
        nh = jnp.tanh(jnp.concatenate([pos_b, seq_hidden], axis=-1) @ w1)
        nh = jax.nn.sigmoid(nh @ glu1_w.T + glu1_b + (hs @ glu2_w.T)[:, None, :])
        beta = nh @ w2 * mask
        sess_emb = jnp.sum(beta * seq_hidden, axis=1)
        select = W_K * _l2norm(sess_emb)
        scores = select @ _l2norm(graph_item_embs).T
        return scores
    y = _L0_rec_ref(r_items, r_inputs, r_alias_inputs, L0_rec_adj_row, L0_rec_adj_col, L0_rec_adj_val, L0_rec_E, L0_rec_pos_emb, L0_rec_w1, L0_rec_w2, L0_rec_glu1_w, L0_rec_glu1_b, L0_rec_glu2_w)
    return y

_drawn_inputs = setup_inputs


def setup_inputs(seed=0):
    import zlib

    import numpy as np

    out = dict(_drawn_inputs(seed))
    spreads = {'L0_rec_glu1_b': (0.0, 0.8)}
    factors = {'L0_rec_pos_emb': 8.0,
     'L0_rec_w1': 7.682,
     'L0_rec_w2': 4.962,
     'L0_rec_glu1_w': 6.445,
     'L0_rec_glu2_w': 26.916}
    for name, (base, spread) in spreads.items():
        noise = np.random.default_rng([zlib.crc32(name.encode()), seed]).standard_normal(out[name].shape)
        drawn = base * np.exp(spread * noise) if base else spread * noise
        out[name] = jnp.asarray(drawn.astype(out[name].dtype))
    for name, factor in factors.items():
        out[name] = (out[name] * factor).astype(out[name].dtype)
    return out
```

```python
import concourse.bass as bass
from concourse import mybir
from concourse.alu_op_type import AluOpType as ALU
from contextlib import ExitStack

F32, I32 = mybir.dt.float32, mybir.dt.int32
ACT = mybir.ActivationFunctionType
AX = mybir.AxisListType

LAYERS = 2
W_K = 12.0
EPS = 1e-12


def session_graph_scores(nc, items, inputs, alias, adj_row, adj_col, adj_val, E, pos_emb,
                         w1, w2, glu1_w, glu1_b, glu2_w, scores):
    P = 128
    N, D = E.shape
    B, L = items.shape
    NNZ = adj_row.shape[0]
    assert D == P and B % P == 0

    Q = 8
    GE = P * Q
    FULL = NNZ // GE
    TAIL = NNZ - FULL * GE
    TP = TAIL // Q
    NG = FULL + 1
    SETS = 3
    ITERS = FULL // SETS
    assert TP * Q == TAIL and TAIL > 0 and FULL % SETS == 0 and TP < P
    W = P
    NB = -(-N // P)
    NP_ = NB * P
    LASTB = N - (NB - 1) * P
    QB = 4
    QUADS = -(-NB // QB)

    NBATCH = B // P
    LQ = -(-L // QB)
    ST = 500
    TILES_PER_STORE = 5
    SW = ST * TILES_PER_STORE
    STORES = N // SW
    assert STORES * SW == N

    def quad(q, total):
        return range(q * QB, min(q * QB + QB, total))

    h1_dram = nc.dram_tensor("h1_scratch", (NP_, D), F32, kind="Internal").ap()
    g_dram = nc.dram_tensor("g_scratch", (NP_, D), F32, kind="Internal").ap()

    with ExitStack() as ctx:
        def sb(name, shape, dt=F32):
            return ctx.enter_context(nc.sbuf_tensor(name, shape, dt))

        def ps(name, shape=(P, 512)):
            return ctx.enter_context(nc.psum_tensor(name, list(shape), F32))

        def sem(name):
            return ctx.enter_context(nc.semaphore(name))

        accT = sb("accT", [P, N + W])
        gnat = sb("gnat", [P, NB, D])
        arena = sb("arena", [P, 2 * SETS * Q * D + 3 * NG * Q])
        o = SETS * Q * D
        gath = arena[:, 0:o].rearrange("p (s d) -> p s d", d=D)
        sel = arena[:, o:2 * o].rearrange("p (s w) -> p s w", w=W)
        rowrel = arena[:, 2 * o:2 * o + NG * Q]
        val = arena[:, 2 * o + NG * Q:2 * o + 2 * NG * Q]
        col = arena[:, 2 * o + 2 * NG * Q:2 * o + 3 * NG * Q].bitcast(I32)
        row_i = sel[:, :, :].rearrange("p s w -> p (s w)")[:, 0:NG * Q].bitcast(I32)
        nhT = arena[:, 0:L * P]
        stages = sb("stages", [P, 2, SW])
        idx_ring = sb("idx_ring", [P, SETS, Q], I32)
        first_i = sb("first_i", [P, NG], I32)
        last_i = sb("last_i", [1, NG], I32)
        span_i = sb("span_i", [1, NG], I32)
        nwin_i = sb("nwin_i", [1, NG], I32)
        nmax_i = sb("nmax_i", [1, 1], I32)
        rowm = sb("rowm", [P, Q])
        iota = sb("iota", [P, P])
        ident = sb("ident", [P, P])
        ones = sb("ones", [P, P])
        hst = sb("hst", [P, 2, QB, D])
        iota_i = hst[:, 1, 1, :].bitcast(I32)
        item_i = sb("item_i", [P, NBATCH, L], I32)
        inp_i = sb("inp_i", [P, NBATCH, L], I32)
        ali_i = sb("ali_i", [P, NBATCH, L], I32)
        item_f = sb("item_f", [P, NBATCH, L])
        neg_f = sb("neg_f", [P, NBATCH, L])
        ali_f = sb("ali_f", [P, NBATCH, L])
        pick = neg_f
        cidx_f = sb("cidx_f", [P, NBATCH, L])
        mask = sb("mask", [P, NBATCH, L])
        cidx = sb("cidx", [P, NBATCH + 2, L], I32)
        sidx = sb("sidx", [P, 2, L], I32)
        cnt = sb("cnt", [P, NBATCH])
        rcnt = sb("rcnt", [P, NBATCH])
        w1_sb = sb("w1_sb", [P, 2, D])
        pos_sb = hst[0:L, 1, 0, :]
        posT = sb("posT", [P, L])
        pw = sb("pw", [P, L])
        glu_sb = hst[:, 0, 0:2, :]
        gluT = sb("gluT", [P, 2, D])
        b1 = sb("b1", [P, 1])
        w2_sb = sb("w2_sb", [P, 1])
        seqb = sb("seqb", [P, L, D])
        seqT = arena[:, L * P:(L + 2 * QB) * P].rearrange("p (k n) -> p k n", k=2)
        u = arena[:, (L + 2 * QB) * P:(L + 4 * QB) * P].rearrange("p (k n) -> p k n", k=2)
        hs = arena[:, (L + 4 * QB + 0) * P:(L + 4 * QB + 1) * P]
        hsn = arena[:, (L + 4 * QB + 1) * P:(L + 4 * QB + 2) * P]
        hsT = arena[:, (L + 4 * QB + 2) * P:(L + 4 * QB + 3) * P]
        gb = arena[:, (L + 4 * QB + 3) * P:(L + 4 * QB + 4) * P]
        ss = sb("ss", [P, 2, QB])
        nrm = sb("nrm", [P, 2, QB])
        rn = sb("rn", [P, 2, QB])
        rns = sb("rns", [P, 2, QB])
        beta = sb("beta", [P, L])
        sess = arena[:, (L + 4 * QB + 4) * P:(L + 4 * QB + 5) * P]
        sn = sb("sn", [P, 4])
        selT = arena[:, (L + 4 * QB + 5) * P:(L + 4 * QB + 6) * P]
        seqs = [seqb[:, :, :], gnat[:, 0:L, :]]

        pw_ps = [ps(f"pw_ps{j}") for j in range(SETS)]
        pt = [ps(f"pt{j}") for j in range(2)]
        py = [ps(f"py{j}") for j in range(2)]
        pm = ps("pm")

        loaded = {k: sem("loaded_" + k) for k in
                  ("rows", "cols", "vals", "first", "last", "E", "sess", "weights")}
        idx_ready = [sem(f"idx_ready{j}") for j in range(SETS)]
        landed = [sem(f"landed{s}") for s in range(SETS * Q)]
        sel_ready = [sem(f"sel_ready{j}") for j in range(SETS)]
        summed = [sem(f"summed{j}") for j in range(SETS)]
        acc_done = sem("acc_done")
        pool_go = sem("pool_go")
        pe_go = sem("pe_go")
        pool_const = sem("pool_const")
        tail_clear = sem("tail_clear")
        consts_ready = sem("consts_ready")
        vchain = sem("vchain")
        tables_ready = sem("tables_ready")
        wt_ps = sem("wt_ps")
        wt_sb = sem("wt_sb")
        acc_complete = sem("acc_complete")
        sl_idx = sem("sl_idx")
        sl_landed = [sem(f"sl_landed{k}") for k in range(Q)]
        sl_sel = sem("sl_sel")
        sl_sum = sem("sl_sum")
        sl_group = sem("sl_group")
        n_T = sem("n_T")
        n_ss = sem("n_ss")
        n_sqrt = sem("n_sqrt")
        n_rn = sem("n_rn")
        n_h = sem("n_h")
        n_add = sem("n_add")
        h_stored = [sem(f"h_stored{k}") for k in range(2)]
        g_stored = sem("g_stored")
        q_ss = sem("q_ss")
        q_sqrt = sem("q_sqrt")
        q_rn = sem("q_rn")
        q_gn = sem("q_gn")
        q_T = sem("q_T")
        q_put = sem("q_put")
        seq_free = [sem(f"seq_free{k}") for k in range(2)]
        got = [[sem(f"got{k}_{t}") for t in range(LQ)] for k in range(2)]
        s_T = sem("s_T")
        s_cp = sem("s_cp")
        s_y = sem("s_y")
        s_nh = sem("s_nh")
        s_hs = sem("s_hs")
        s_hsT = sem("s_hsT")
        s_hsc = sem("s_hsc")
        s_gp = sem("s_gp")
        s_gb = sem("s_gb")
        s_z = sem("s_z")
        s_u = sem("s_u")
        s_th = sem("s_th")
        s_beta = sem("s_beta")
        s_sess = sem("s_sess")
        s_sq = sem("s_sq")
        s_sel = sem("s_sel")
        s_selT = sem("s_selT")
        s_selc = sem("s_selc")
        s_sc = sem("s_sc")
        s_st = sem("s_st")
        s_out = [sem(f"s_out{k}") for k in range(2)]

        block = ctx.enter_context(nc.Block())

        def uses(layer, j):
            return layer * (ITERS + (1 if j == 0 else 0))

        ACC0 = 4

        def acc_value(layer):
            return ACC0 + layer * (NG + 1)

        def used(layer, j):
            return layer * (ITERS + (1 if j == 0 else 0))

        ACC0 = SETS + 1

        def acc_at(layer, g):
            return ACC0 + layer * (NG + 1) + g

        H_STORES = [-(-QUADS // 2), QUADS // 2]
        FULLQ = (QUADS - 1) // 2
        LASTN = NB - (QUADS - 1) * QB
        assert QUADS % 2 == 1

        @block.sync
        def _(sp):
            body = FULL * GE

            def edges(src, dst, s):
                sp.dma_start(dst[:, 0:FULL * Q].rearrange("p (g q) -> p g q", q=Q),
                             src[0:body].rearrange("(g p q) -> p g q", p=P, q=Q)).then_inc(s, 16)
                sp.dma_start(dst[0:TP, FULL * Q:NG * Q],
                             src[body:NNZ].rearrange("(p q) -> p q", q=Q)).then_inc(s, 16)

            first = adj_row[0:body].rearrange("(g n) -> g n", n=GE)
            sp.wait_ge(tail_clear, 1)
            edges(adj_col, col, loaded["cols"])
            edges(adj_row, row_i, loaded["rows"])
            sp.dma_start(first_i[:, 0:FULL], first[:, 0:1].rearrange("g o -> o g").broadcast_to([P, FULL]),
                         allow_slow_non_contiguous=True).then_inc(loaded["first"], 16)
            sp.dma_start(first_i[:, FULL:NG], adj_row[body:body + 1].rearrange("(o n) -> o n", o=1)
                         .broadcast_to([P, 1]), allow_slow_non_contiguous=True).then_inc(loaded["first"], 16)
            edges(adj_val, val, loaded["vals"])
            sp.dma_start(last_i[0:1, 0:FULL], first[:, GE - 1:GE].rearrange("g o -> o g"),
                         allow_slow_non_contiguous=True).then_inc(loaded["last"], 16)
            sp.dma_start(last_i[0:1, FULL:NG], adj_row[NNZ - 1:NNZ].rearrange("(o n) -> o n", o=1)
                         ).then_inc(loaded["last"], 16)
            sp.dma_start(w1_sb[:, :, :], w1.rearrange("(h p) e -> p h e", p=P)).then_inc(loaded["weights"], 16)
            sp.dma_start(pos_sb[:, :], pos_emb).then_inc(loaded["weights"], 16)
            sp.dma_start(glu_sb[:, 0, :], glu1_w).then_inc(loaded["weights"], 16)
            sp.dma_start(glu_sb[:, 1, :], glu2_w).then_inc(loaded["weights"], 16)
            sp.dma_start(b1[:, :], glu1_b.rearrange("(p o) -> p o", o=1)).then_inc(loaded["weights"], 16)
            sp.dma_start(w2_sb[:, :], w2).then_inc(loaded["weights"], 16)
            for dst, src in ((item_i, items), (inp_i, inputs), (ali_i, alias)):
                sp.dma_start(dst[:, :, :], src.rearrange("(b p) l -> p b l", p=P)).then_inc(loaded["sess"], 16)
            sp.dma_start(gnat[:, 0:NB - 1, :],
                         E[0:(NB - 1) * P, :].rearrange("(b p) d -> p b d", p=P)).then_inc(loaded["E"], 16)
            sp.dma_start(gnat[0:LASTB, NB - 1, :], E[(NB - 1) * P:N, :]).then_inc(loaded["E"], 16)

            def rows_of(dram, row0, n):
                return dram[bass.ds(row0, n * P), :].rearrange("(b p) d -> p b d", p=P)

            with sp.Fori(0, FULLQ) as i:
                for k in range(2):
                    q = 2 * i + k
                    sp.wait_ge(n_h, q + 1)
                    sp.dma_start(rows_of(h1_dram, q * (QB * P), QB), hst[:, k, :, :]).then_inc(h_stored[k], 16)
            sp.wait_ge(n_h, QUADS)
            sp.dma_start(rows_of(h1_dram, (QUADS - 1) * QB * P, LASTN),
                         hst[:, 0, 0:LASTN, :]).then_inc(h_stored[0], 16)
            with sp.Fori(0, FULLQ) as i:
                for k in range(2):
                    q = 2 * i + k
                    sp.wait_ge(n_add, q + 1 + QUADS)
                    sp.dma_start(rows_of(g_dram, q * (QB * P), QB),
                                 gnat[:, bass.ds(q * QB, QB), :]).then_inc(g_stored, 16)
            sp.wait_ge(n_add, 2 * QUADS)
            sp.dma_start(rows_of(g_dram, (QUADS - 1) * QB * P, LASTN),
                         gnat[:, (QUADS - 1) * QB:NB, :]).then_inc(g_stored, 16)

            with sp.Fori(0, NBATCH // 2) as i:
                for h in range(2):
                    for m in range(STORES):
                        n = STORES * h + m
                        sp.wait_ge(s_st, 2 + (i * (2 * STORES) + n + 1) * TILES_PER_STORE)
                        sp.dma_start(scores[bass.ds((2 * i + h) * P, P), m * SW:(m + 1) * SW],
                                     stages[:, n % 2, :]).then_inc(s_out[n % 2], 16)
            for k in range(2):
                sp.wait_ge(s_out[k], 16 * (1 + NBATCH * STORES // 2))

        @block.gpsimd
        def _(pool):
            nc.gpsimd.iota(iota_i[:, :], pattern=[[1, P]], base=0, channel_multiplier=0).then_inc(pool_const, 1)
            nc.gpsimd.memset(ident[:, :], 0.0).then_inc(pool_const, 1)
            pool.wait_ge(pool_const, 2)
            nc.gpsimd.affine_select(out=ident[:, :], in_=ident[:, :], compare_op=ALU.not_equal, fill=1.0,
                                    base=0, pattern=[[-1, P]], channel_multiplier=1).then_inc(pool_const, 1)

            def gather(dst, src, index, s):
                nc.gpsimd.indirect_dma_start(dst, None, src, bass.IndirectOffsetOnAxis(ap=index, axis=0)
                                             ).then_inc(s, 16)

            def gather_group(table, j, use, parts):
                pool.wait_ge(idx_ready[j], use + 1)
                pool.sem_inc(pool_go, 1)
                for k in range(Q):
                    gather(gath[0:parts, j * Q + k, :], table, idx_ring[0:parts, j, k:k + 1], landed[j * Q + k])

            slow_groups = pool.alloc_register("pool_slow_groups")
            pool.reg_mov(slow_groups, 0)

            def slow_gathers(layer, table):
                most = pool.value_load(nmax_i[0:1, 0:1], min_val=0, max_val=NB)
                with pool.If(most > 0):
                    with pool.Fori(0, NG) as g:
                        windows = pool.value_load(nwin_i[0:1, bass.ds(g, 1)], min_val=0, max_val=NB)
                        with pool.If(windows > 0):
                            m = pool.snap(slow_groups, min_val=0, max_val=2 * NG)
                            pool.wait_ge(sl_group, m + 1)
                            nc.gpsimd.tensor_copy(idx_ring[:, 0, :], col[:, bass.ds(g * Q, Q)]).then_inc(sl_idx, 1)
                            pool.wait_ge(sl_idx, m + 1)
                            pool.sem_inc(pool_go, 1)
                            for k in range(Q):
                                gather(gath[:, k, :], table, idx_ring[:, 0, k:k + 1], sl_landed[k])
                            pool.reg_add(slow_groups, slow_groups, 1)

            for layer, table in enumerate((E, h1_dram)):
                if layer:
                    for k in range(2):
                        pool.wait_ge(h_stored[k], 16 * H_STORES[k])
                with pool.Fori(0, ITERS) as i:
                    for j in range(SETS):
                        gather_group(table, j, used(layer, j) + i, P)
                gather_group(table, 0, used(layer, 0) + ITERS, TP)
                if layer == 0:
                    pool.wait_ge(tables_ready, 1)
                pool.wait_ge(acc_done, acc_at(layer, NG))
                slow_gathers(layer, table)

            pool.wait_ge(g_stored, 16 * QUADS)
            with pool.Fori(0, NBATCH // 2) as i:
                for h in range(2):
                    pool.wait_ge(seq_free[h], i + 1)
                    pool.sem_inc(pool_go, 1)
                    for l in range(L):
                        gather(seqs[h][:, l, :], g_dram, sidx[:, h, l:l + 1], got[h][l // QB])

        @block.tensor
        def _(pe):
            mm, tr = nc.tensor.matmul, nc.tensor.transpose
            pe.wait_ge(pool_const, 3)
            pe.wait_ge(loaded["weights"], 16 * 6)
            tr(pm[:, 0:L], pos_sb[:, :], ident[0:L, 0:L])
            for w in range(2):
                last = tr(pm[:, (w + 1) * P:(w + 2) * P], glu_sb[:, w, :], ident[:, :])
            last.then_inc(wt_ps, 1)
            pe.wait_ge(wt_sb, 1)
            mm(pm[:, 3 * P:3 * P + L], w1_sb[:, 0, :], posT[:, :], start=True, stop=True).then_inc(wt_ps, 1)

            def sum_group(j, use, turn, parts):
                pe.wait_ge(sel_ready[j], Q * (use + 1))
                pe.wait_ge(acc_done, turn - SETS + 1)
                for k in range(Q):
                    s = j * Q + k
                    pe.wait_ge(landed[s], 16 * (use + 1))
                    last = mm(pw_ps[j][:, 0:W], gath[0:parts, s, :], sel[0:parts, s, :], start=k == 0, stop=k == Q - 1)
                last.then_inc(summed[j], 1)

            slow_groups = pe.alloc_register("pe_slow_groups")
            slow_windows = pe.alloc_register("pe_slow_windows")
            pe.reg_mov(slow_groups, 0)
            pe.reg_mov(slow_windows, 0)

            def slow_sums(layer):
                pe.wait_ge(tables_ready, 1)
                pe.wait_ge(acc_done, acc_at(layer, NG))
                most = pe.value_load(nmax_i[0:1, 0:1], min_val=0, max_val=NB)
                with pe.If(most > 0):
                    with pe.Fori(0, NG) as g:
                        windows = pe.value_load(nwin_i[0:1, bass.ds(g, 1)], min_val=0, max_val=NB)
                        with pe.If(windows > 0):
                            m = pe.snap(slow_groups, min_val=0, max_val=2 * NG)
                            for k in range(Q):
                                pe.wait_ge(sl_landed[k], 16 * (m + 1))
                            pe.sem_inc(pe_go, 1)
                            with pe.Fori(0, windows):
                                t = pe.snap(slow_windows, min_val=0, max_val=4 * NG)
                                pe.wait_ge(sl_sel, t + 1)
                                for k in range(Q):
                                    last = mm(pw_ps[0][:, 0:W], gath[:, k, :], sel[:, k, :], start=k == 0, stop=k == Q - 1)
                                last.then_inc(sl_sum, 1)
                                pe.reg_add(slow_windows, slow_windows, 1)
                            pe.reg_add(slow_groups, slow_groups, 1)

            for layer in range(LAYERS):
                with pe.Fori(0, ITERS) as i:
                    for j in range(SETS):
                        sum_group(j, used(layer, j) + i, acc_at(layer, 0) + i * SETS + j, P)
                sum_group(0, used(layer, 0) + ITERS, acc_at(layer, FULL), TP)
                slow_sums(layer)
                pe.wait_ge(acc_complete, layer + 1)
                for q in range(QUADS):
                    v = layer * QUADS + q
                    if v >= 2:
                        pe.wait_ge(n_h, v - 1)
                    for b in quad(q, NB):
                        last = tr(pt[q % 2][:, (b - q * QB) * P:(b - q * QB + 1) * P],
                                  accT[:, b * P:(b + 1) * P], ident[:, :])
                    last.then_inc(n_T, 1)

            def items_T(k, v, n):
                pe.wait_ge(q_gn, v + 1)
                for b in range(n):
                    last = tr(pt[k][:, b * P:(b + 1) * P], hst[:, k, b, :], ident[:, :])
                last.then_inc(q_T, 1)

            with pe.Fori(0, FULLQ) as i:
                for k in range(2):
                    items_T(k, 2 * i + k, QB)
            items_T(0, QUADS - 1, LASTN)

            with pe.Fori(0, NBATCH // 2) as i:
                for h in range(2):
                    c0 = i * (2 * LQ) + h * LQ
                    b0 = i * 2 + h
                    for t in range(LQ):
                        r = (h * LQ + t) % 2
                        n = len(quad(t, L))
                        pe.wait_ge(got[h][t], (i + 1) * (16 * n))
                        pe.wait_ge(s_cp, c0 + t + 1)
                        for x, l in enumerate(quad(t, L)):
                            last = tr(pt[r][:, x * P:(x + 1) * P], seqs[h][:, l, :], ident[:, :])
                        last.then_inc(s_T, 1)
                        pe.wait_ge(s_cp, c0 + t + 3)
                        pe.wait_ge(s_nh, c0 + t + 1)
                        mm(py[r][:, 0:n * P], w1_sb[:, 1, :], seqT[:, r, 0:n * P], start=True, stop=True
                           ).then_inc(s_y, 1)
                    pe.wait_ge(s_hs, b0 + 1)
                    tr(pm[:, 0:P], hsn[:, :], ident[:, :]).then_inc(s_hsT, 1)
                    pe.wait_ge(s_hsc, b0 + 1)
                    mm(pm[:, P:2 * P], gluT[:, 1, :], hsT[:, :], start=True, stop=True).then_inc(s_gp, 1)
                    for t in range(LQ):
                        r = (h * LQ + t) % 2
                        n = len(quad(t, L))
                        pe.wait_ge(s_nh, c0 + LQ + 2)
                        pe.wait_ge(s_u, c0 + t + 1)
                        mm(py[r][:, 0:n * P], gluT[:, 0, :], nhT[:, t * QB * P:(t * QB + n) * P],
                           start=True, stop=True).then_inc(s_z, 1)
                    for t in range(LQ):
                        pe.wait_ge(s_th, c0 + t + 1)
                        for l in quad(t, L):
                            last = mm(pm[:, 2 * P + l:2 * P + l + 1], nhT[:, l * P:(l + 1) * P], w2_sb[:, :],
                                      start=True, stop=True)
                    last.then_inc(s_beta, 1)
                    pe.wait_ge(s_sel, b0 + 1)
                    tr(pm[:, 3 * P:4 * P], sess[:, :], ident[:, :]).then_inc(s_selT, 1)
                    pe.wait_ge(s_selc, b0 + 1)
                    for m in range(STORES * TILES_PER_STORE):
                        c = h * STORES * TILES_PER_STORE + m
                        pe.wait_ge(s_st, i * (2 * STORES * TILES_PER_STORE) + c + 1)
                        mm(pw_ps[c % 2][:, 0:ST], selT[:, :], accT[:, m * ST:(m + 1) * ST], start=True, stop=True
                           ).then_inc(s_sc, 1)

        @block.scalar
        def _(act):
            def columns(j, use, g):
                act.wait_ge(summed[j], use + 1)
                nc.scalar.copy(idx_ring[:, j, :], col[:, bass.ds(g * Q, Q)]).then_inc(idx_ready[j], 1)

            def norms(src, k, n, v, got_ss, got_root):
                for b in range(n):
                    last = nc.scalar.activation(py[0][:, b * D:(b + 1) * D], src(b), ACT.Square, accum_out=ss[:, k, b:b + 1])
                    last.then_inc(got_ss, 1)
                act.wait_ge(got_ss, v)
                nc.scalar.activation(nrm[:, k, 0:n], ss[:, k, 0:n], ACT.Sqrt).then_inc(got_root, 1)

            act.wait_ge(loaded["cols"], 32)
            for layer in range(LAYERS):
                with act.Fori(0, ITERS) as i:
                    for j in range(SETS):
                        columns(j, used(layer, j) + i, i * SETS + j)
                columns(0, used(layer, 0) + ITERS, FULL)

                def row_norms(k, q, n, v):
                    act.wait_ge(n_T, q + 1)
                    norms(lambda b: pt[k][:, b * P:(b + 1) * P], k, n, v, n_ss, n_sqrt)

                with act.Fori(0, FULLQ) as i:
                    for k in range(2):
                        q = 2 * i + k
                        row_norms(k, q + layer * QUADS, QB, q * QB + (layer * NB + QB))
                row_norms(0, (layer + 1) * QUADS - 1, LASTN, (layer + 1) * NB)

            def item_norms(k, q, q0, n, v):
                act.wait_ge(q_rn, q + 1)
                norms(lambda b: gnat[:, bass.ds(q0 + b, 1), :].rearrange("p o d -> p (o d)"), k, n, v, q_ss, q_sqrt)

            act.wait_ge(n_add, 2 * QUADS)
            with act.Fori(0, FULLQ) as i:
                for k in range(2):
                    q = 2 * i + k
                    item_norms(k, q, q * QB, QB, q * QB + QB)
            item_norms(0, QUADS - 1, (QUADS - 1) * QB, LASTN, NB)

            with act.Fori(0, NBATCH // 2) as i:
                for h in range(2):
                    c0 = i * (2 * LQ) + h * LQ
                    b0 = i * 2 + h
                    for t in range(LQ):
                        r = (h * LQ + t) % 2
                        act.wait_ge(s_y, c0 + t + 1)
                        for x, l in enumerate(quad(t, L)):
                            last = nc.scalar.activation(nhT[:, l * P:(l + 1) * P], py[r][:, x * P:(x + 1) * P],
                                                        ACT.Tanh, bias=pw[:, L - 1 - l:L - l])
                        last.then_inc(s_nh, 1)
                    for t in range(LQ):
                        r = (h * LQ + t) % 2
                        n = len(quad(t, L))
                        act.wait_ge(s_u, c0 + t + 3)
                        nc.scalar.activation(nhT[:, t * QB * P:(t * QB + n) * P], u[:, r, 0:n * P],
                                             ACT.Sigmoid).then_inc(s_th, 1)
                    act.wait_ge(s_sess, b0 + 1)
                    nc.scalar.activation(pw_ps[2][:, 0:D], sess[:, :], ACT.Square, accum_out=sn[:, 0:1]).then_inc(s_sq, 1)
                    act.wait_ge(s_sq, 2 * b0 + 1)
                    nc.scalar.activation(sn[:, 1:2], sn[:, 0:1], ACT.Sqrt).then_inc(s_sq, 1)
                    for m in range(STORES * TILES_PER_STORE):
                        c = h * STORES * TILES_PER_STORE + m
                        n = c // TILES_PER_STORE
                        if c % TILES_PER_STORE == 0:
                            act.wait_ge(s_out[n % 2], (i * STORES + n // 2 + 1) * 16)
                        act.wait_ge(s_sc, i * (2 * STORES * TILES_PER_STORE) + c + 1)
                        at = (c % TILES_PER_STORE) * ST
                        nc.scalar.copy(stages[:, n % 2, at:at + ST], pw_ps[c % 2][:, 0:ST]).then_inc(s_st, 1)

        @block.vector
        def _(dve):
            v = nc.vector
            steps = [0]

            def link(ins):
                steps[0] += 1
                ins.then_inc(vchain, 1)
                dve.wait_ge(vchain, steps[0])

            def mark(ins):
                steps[0] += 1
                ins.then_inc(vchain, 1)

            mark(v.memset(col[:, FULL * Q:NG * Q], 0))
            mark(v.memset(val[:, FULL * Q:NG * Q], 0.0))
            mark(v.memset(rowrel[:, FULL * Q:NG * Q], -1.0))
            link(v.memset(gnat[:, NB - 1, :], 0.0))
            dve.sem_inc(tail_clear, 1)
            for j in range(SETS):
                dve.sem_inc(summed[j], 1)
            dve.sem_inc(acc_done, SETS)
            dve.sem_inc(sl_group, 1)
            v.memset(accT[:, :], 0.0).then_inc(acc_done, 1)
            mark(v.memset(cidx_f[:, :, :], 0.0))
            mark(v.memset(cidx[:, NBATCH:NBATCH + 2, :], 0))
            dve.wait_ge(pool_const, 1)
            mark(v.tensor_copy(iota[:, :], iota_i[:, :]))
            dve.wait_ge(loaded["rows"], 32)
            dve.wait_ge(loaded["first"], 32)
            mark(v.tensor_tensor(rowrel[:, 0:FULL * Q].rearrange("p (g q) -> p g q", q=Q),
                                 row_i[:, 0:FULL * Q].rearrange("p (g q) -> p g q", q=Q),
                                 first_i[:, 0:FULL].unsqueeze(2).broadcast_to([P, FULL, Q]), ALU.subtract))
            link(v.tensor_tensor(rowrel[0:TP, FULL * Q:NG * Q], row_i[0:TP, FULL * Q:NG * Q],
                                 first_i[0:TP, FULL:NG].broadcast_to([TP, Q]), ALU.subtract))
            dve.wait_ge(loaded["last"], 32)
            link(v.tensor_tensor(span_i[:, :], last_i[:, :], first_i[0:1, :], ALU.subtract))
            link(v.tensor_scalar(nwin_i[:, :], span_i[:, :], 7, None, ALU.arith_shift_right))
            link(v.tensor_reduce(nmax_i[:, :], nwin_i[:, :], AX.X, ALU.max))
            dve.sem_inc(tables_ready, 1)
            dve.wait_ge(wt_ps, 1)
            mark(v.tensor_copy(posT[:, :], pm[:, 0:L]))
            link(v.tensor_copy(gluT[:, :, :], pm[:, P:3 * P].rearrange("p (w f) -> p w f", w=2)))
            dve.sem_inc(wt_sb, 1)
            dve.wait_ge(wt_ps, 2)
            link(v.tensor_copy(pw[:, :], pm[:, 3 * P:3 * P + L]))
            dve.wait_ge(loaded["sess"], 48)
            mark(v.tensor_copy(item_f[:, :, :], item_i[:, :, :]))
            mark(v.tensor_copy(ali_f[:, :, :], ali_i[:, :, :]))
            link(v.tensor_scalar(mask[:, :, :], inp_i[:, :, :], 0.0, None, ALU.not_equal))
            mark(v.tensor_reduce(cnt[:, :], mask[:, :, :], AX.X, ALU.add))
            link(v.tensor_scalar(neg_f[:, :, :], item_f[:, :, :], 0.0, float(N), ALU.is_lt, ALU.mult))
            mark(v.reciprocal(rcnt[:, :], cnt[:, :]))
            link(v.tensor_tensor(item_f[:, :, :], item_f[:, :, :], neg_f[:, :, :], ALU.add))
            link(v.tensor_scalar(item_f[:, :, :], item_f[:, :, :], 0.0, float(N - 1), ALU.max, ALU.min))
            dve.wait_ge(loaded["vals"], 32)

            def add_group(layer, j, use, g, parts):
                row0 = dve.value_load(first_i[0:1, bass.ds(g, 1)], min_val=0, max_val=N - 1)
                dve.wait_ge(summed[j], use + 1)
                for k in range(Q):
                    v.tensor_scalar(sel[0:parts, j * Q + k, :], iota[0:parts, :], rowrel[0:parts, bass.ds(g * Q + k, 1)],
                                    val[0:parts, bass.ds(g * Q + k, 1)], ALU.is_equal, ALU.mult
                                    ).then_inc(sel_ready[j], 1)
                dve.wait_ge(summed[j], use + 2)
                dve.wait_ge(acc_done, acc_at(layer, 0) + g)
                v.tensor_tensor(accT[:, bass.ds(row0, W)], accT[:, bass.ds(row0, W)], pw_ps[j][:, 0:W], ALU.add
                                ).then_inc(acc_done, 1)

            slow_windows = dve.alloc_register("dve_slow_windows")
            dve.reg_mov(slow_windows, 0)
            place = dve.alloc_register("dve_window_row")

            def slow_adds():
                most = dve.value_load(nmax_i[0:1, 0:1], min_val=0, max_val=NB)
                with dve.If(most > 0):
                    with dve.Fori(0, NG) as g:
                        windows = dve.value_load(nwin_i[0:1, bass.ds(g, 1)], min_val=0, max_val=NB)
                        with dve.If(windows > 0):
                            row0 = dve.value_load(first_i[0:1, bass.ds(g, 1)], min_val=0, max_val=N - 1)
                            v.tensor_copy(rowm[:, :], rowrel[:, bass.ds(g * Q, Q)])
                            dve.drain()
                            dve.reg_mov(place, row0)
                            with dve.Fori(0, windows):
                                v.tensor_scalar(rowm[:, :], rowm[:, :], float(W), None, ALU.subtract)
                                dve.drain()
                                for k in range(Q):
                                    v.tensor_scalar(sel[:, k, :], iota[:, :], rowm[:, k:k + 1],
                                                    val[:, bass.ds(g * Q + k, 1)], ALU.is_equal, ALU.mult)
                                dve.drain()
                                dve.sem_inc(sl_sel, 1)
                                t = dve.snap(slow_windows, min_val=0, max_val=4 * NG)
                                dve.wait_ge(sl_sum, t + 1)
                                dve.reg_add(place, place, W)
                                here = dve.snap(place, min_val=W, max_val=N - 1)
                                dst = accT[:, bass.ds(here, W)]
                                v.tensor_tensor(dst, dst, pw_ps[0][:, 0:W], ALU.add)
                                dve.drain()
                                dve.reg_add(slow_windows, slow_windows, 1)
                            dve.sem_inc(sl_group, 1)

            def layer_rows(layer, k, q, q0, n, weight, spare):
                dve.wait_ge(n_sqrt, q + 1)
                v.tensor_scalar(rn[:, k, 0:n], nrm[:, k, 0:n], EPS, None, ALU.max).then_inc(n_rn, 1)
                dve.wait_ge(n_rn, 3 * q + 1)
                v.reciprocal(rns[:, k, 0:n], rn[:, k, 0:n]).then_inc(n_rn, 1)
                dve.wait_ge(n_rn, 3 * q + 2)
                v.tensor_scalar(rn[:, k, 0:n], rns[:, k, 0:n], weight, None, ALU.mult).then_inc(n_rn, 1)
                dve.wait_ge(n_rn, 3 * q + 3)
                if spare is not None:
                    dve.wait_ge(h_stored[k], spare)
                v.tensor_tensor(hst[:, k, 0:n, :], pt[k][:, 0:n * P].rearrange("p (b d) -> p b d", b=n),
                                rn[:, k, 0:n].unsqueeze(2).broadcast_to([P, n, D]), ALU.mult).then_inc(n_h, 1)
                dve.wait_ge(n_h, q + 1)
                items_ = gnat[:, bass.ds(q0, n), :]
                v.scalar_tensor_tensor(items_, items_, weight, hst[:, k, 0:n, :], ALU.mult, ALU.add).then_inc(n_add, 1)

            for layer in range(LAYERS):
                if layer:
                    v.memset(accT[:, :], 0.0).then_inc(acc_done, 1)
                if layer == 0:
                    c0 = steps[0]
                    with dve.Fori(0, L) as i:
                        for j in range(SETS):
                            add_group(layer, j, used(layer, j) + i, i * SETS + j, P)
                        here = item_f[:, :, bass.ds(i, 1)].broadcast_to([P, NBATCH, L])
                        v.scalar_tensor_tensor(pick[:, :, :], ali_f[:, :, :], 0.0, here, ALU.is_equal, ALU.mult
                                               ).then_inc(vchain, 1)
                        dve.wait_ge(vchain, i * 3 + (c0 + 1))
                        v.tensor_tensor(cidx_f[:, :, :], cidx_f[:, :, :], pick[:, :, :], ALU.add).then_inc(vchain, 1)
                        v.tensor_scalar(ali_f[:, :, :], ali_f[:, :, :], -1.0, None, ALU.add).then_inc(vchain, 1)
                        dve.wait_ge(vchain, i * 3 + (c0 + 3))
                    steps[0] += 3 * L
                    start = L
                else:
                    start = 0
                with dve.Fori(start, ITERS) as i:
                    for j in range(SETS):
                        add_group(layer, j, used(layer, j) + i, i * SETS + j, P)
                add_group(layer, 0, used(layer, 0) + ITERS, FULL, TP)
                if layer == 0:
                    link(v.tensor_copy(cidx[:, 0:NBATCH, :], cidx_f[:, :, :]))
                    link(v.tensor_copy(sidx[:, :, :], cidx[:, 0:2, :]))
                    dve.wait_ge(loaded["E"], 32)
                dve.wait_ge(acc_done, acc_at(layer, NG))
                slow_adds()
                dve.drain()
                dve.sem_inc(acc_complete, 1)

                weight = 1.0 if layer < LAYERS - 1 else 1.0 / (LAYERS + 1)
                if layer:
                    for k in range(2):
                        dve.wait_ge(h_stored[k], 16 * H_STORES[k])
                if layer == 0:
                    for k in range(2):
                        layer_rows(layer, k, k, k * QB, QB, weight, None)
                with dve.Fori(1 if layer == 0 else 0, FULLQ) as i:
                    for k in range(2):
                        q = 2 * i + k
                        layer_rows(layer, k, q + layer * QUADS, q * QB, QB, weight, i * 16 if layer == 0 else None)
                layer_rows(layer, 0, (layer + 1) * QUADS - 1, (QUADS - 1) * QB, LASTN, weight,
                           FULLQ * 16 if layer == 0 else None)

            dve.sem_inc(q_rn, 2)
            dve.sem_inc(seq_free[0], 1)
            dve.wait_ge(n_add, 2 * QUADS)

            def item_rows(k, q, q0, n):
                dve.wait_ge(q_sqrt, q + 1)
                v.tensor_scalar(rn[:, k, 0:n], nrm[:, k, 0:n], EPS, None, ALU.max).then_inc(q_rn, 1)
                dve.wait_ge(q_rn, q + 3)
                v.reciprocal(rns[:, k, 0:n], rn[:, k, 0:n]).then_inc(vchain, 1)
                dve.wait_ge(vchain, q + (steps[0] + 1))
                v.tensor_tensor(hst[:, k, 0:n, :], gnat[:, bass.ds(q0, n), :],
                                rns[:, k, 0:n].unsqueeze(2).broadcast_to([P, n, D]), ALU.mult).then_inc(q_gn, 1)
                dve.wait_ge(q_T, q + 1)
                v.tensor_copy(accT[:, bass.ds(q0 * P, n * P)], pt[k][:, 0:n * P]).then_inc(q_put, 1)

            with dve.Fori(0, FULLQ) as i:
                for k in range(2):
                    item_rows(k, 2 * i + k, (2 * i + k) * QB, QB)
            item_rows(0, QUADS - 1, (QUADS - 1) * QB, LASTN)
            steps[0] += QUADS
            dve.wait_ge(g_stored, 16 * QUADS)
            dve.wait_ge(q_put, QUADS)
            dve.sem_inc(seq_free[1], 1)
            for s in (s_cp, s_nh, s_u, s_st):
                dve.sem_inc(s, 2)
            for k in range(2):
                dve.sem_inc(s_out[k], 16)

            link_c = steps[0]
            PER = 2 * L + 5

            with dve.Fori(0, NBATCH // 2) as i:
                for h in range(2):
                    c0 = i * (2 * LQ) + h * LQ
                    b0 = i * 2 + h
                    own = [0]

                    def step(ins):
                        own[0] += 1
                        ins.then_inc(vchain, 1)
                        dve.wait_ge(vchain, i * (2 * PER) + (link_c + h * PER + own[0]))

                    for t in range(LQ):
                        r = (h * LQ + t) % 2
                        n = len(quad(t, L))
                        dve.wait_ge(s_T, c0 + t + 1)
                        v.tensor_copy(seqT[:, r, 0:n * P], pt[r][:, 0:n * P]).then_inc(s_cp, 1)
                        for l in quad(t, L):
                            m = mask[:, bass.ds(b0, 1), l:l + 1].rearrange("p o l -> p (o l)")
                            if l == 0:
                                step(v.tensor_scalar(hs[:, :], seqs[h][:, l, :], m, None, ALU.mult))
                            else:
                                step(v.scalar_tensor_tensor(hs[:, :], seqs[h][:, l, :], m, hs[:, :], ALU.mult, ALU.add))
                    v.tensor_scalar(hsn[:, :], hs[:, :], rcnt[:, bass.ds(b0, 1)], None, ALU.mult).then_inc(s_hs, 1)
                    dve.wait_ge(s_hsT, b0 + 1)
                    v.tensor_copy(hsT[:, :], pm[:, 0:P]).then_inc(s_hsc, 1)
                    dve.wait_ge(s_gp, b0 + 1)
                    step(v.tensor_scalar(gb[:, :], pm[:, P:2 * P], b1[:, 0:1], None, ALU.add))
                    for t in range(LQ):
                        r = (h * LQ + t) % 2
                        n = len(quad(t, L))
                        dve.wait_ge(s_z, c0 + t + 1)
                        if t >= 2:
                            dve.wait_ge(s_th, c0 + t - 1)
                        v.tensor_tensor(u[:, r, 0:n * P].rearrange("p (x b) -> p x b", x=n),
                                        py[r][:, 0:n * P].rearrange("p (x b) -> p x b", x=n),
                                        gb[:, :].unsqueeze(1).broadcast_to([P, n, P]), ALU.add).then_inc(s_u, 1)
                    dve.wait_ge(s_beta, b0 + 1)
                    step(v.tensor_tensor(beta[:, :], pm[:, 2 * P:2 * P + L],
                                         mask[:, bass.ds(b0, 1), :].rearrange("p o l -> p (o l)"), ALU.mult))
                    for l in range(L):
                        m = beta[:, l:l + 1]
                        if l == 0:
                            ins = v.tensor_scalar(sess[:, :], seqs[h][:, l, :], m, None, ALU.mult)
                        else:
                            ins = v.scalar_tensor_tensor(sess[:, :], seqs[h][:, l, :], m, sess[:, :], ALU.mult, ALU.add)
                        step(ins)
                    dve.sem_inc(s_sess, 1)
                    step(v.tensor_copy(sidx[:, h, :], cidx[:, bass.ds(b0 + 2, 1), :].rearrange("p o l -> p (o l)")))
                    dve.sem_inc(seq_free[h], 1)
                    dve.wait_ge(s_sq, 2 * b0 + 2)
                    step(v.tensor_scalar(sn[:, 2:3], sn[:, 1:2], EPS, None, ALU.max))
                    step(v.reciprocal(sn[:, 3:4], sn[:, 2:3]))
                    assert own[0] == PER
                    v.tensor_scalar(sess[:, :], sess[:, :], sn[:, 3:4], W_K, ALU.mult, ALU.mult).then_inc(s_sel, 1)
                    dve.wait_ge(s_selT, b0 + 1)
                    v.tensor_copy(selT[:, :], pm[:, 3 * P:4 * P]).then_inc(s_selc, 1)


_INS = ["r_items", "r_inputs", "r_alias_inputs", "L0_rec_adj_row", "L0_rec_adj_col", "L0_rec_adj_val",
        "L0_rec_E", "L0_rec_pos_emb", "L0_rec_w1", "L0_rec_w2", "L0_rec_glu1_w", "L0_rec_glu1_b", "L0_rec_glu2_w"]


def kernel(**inputs):
    import numpy as np
    import concourse.bacc as bacc
    from concourse.bass_utils import run_bass_kernel_spmd

    nc = bacc.Bacc("TRN2", target_bir_lowering=False, num_devices=1)
    arrays, args = {}, []
    for name in _INS:
        a = np.ascontiguousarray(inputs[name])
        arrays[f"in_{name}"] = a
        args.append(nc.dram_tensor(f"in_{name}", a.shape, mybir.dt.from_np(a.dtype), kind="ExternalInput").ap())
    shape = (inputs["r_items"].shape[0], inputs["L0_rec_E"].shape[0])
    scores = nc.dram_tensor("scores", shape, F32, kind="ExternalOutput").ap()
    session_graph_scores(nc, *args, scores)
    r = run_bass_kernel_spmd(nc, [arrays], core_ids=[0])
    return r.results[0]["scores"]
```

```python
import concourse.bass as bass
from concourse import mybir
from concourse.alu_op_type import AluOpType as ALU
from contextlib import ExitStack

F32, I32, F16 = mybir.dt.float32, mybir.dt.int32, mybir.dt.float16
ACT = mybir.ActivationFunctionType
AX = mybir.AxisListType

LAYERS = 2
W_K = 12.0
EPS = 1e-12
ITEM_SCALE = 2.0 ** 12
SELECT_SCALE = 2.0 ** 10


def session_graph_scores(nc, items, inputs, alias, adj_row, adj_col, adj_val, E, pos_emb,
                         w1, w2, glu1_w, glu1_b, glu2_w, scores):
    P = 128
    N, D = E.shape
    B, L = items.shape
    NNZ = adj_row.shape[0]
    assert D == P and B % P == 0

    Q = 8
    GE = P * Q
    FULL = NNZ // GE
    TAIL = NNZ - FULL * GE
    TP = TAIL // Q
    NG = FULL + 1
    SETS = 3
    ITERS = FULL // SETS
    EARLY = 4
    EG = EARLY * SETS + 1
    assert TP * Q == TAIL and TAIL > 0 and FULL % SETS == 0 and TP < P
    W = P
    QB = 4
    QR = QB * P
    QUADS = -(-N // QR)
    NB = QUADS * QB
    NPAD = NB * P
    FB = N // P
    LASTB = N - FB * P
    assert LAYERS == 2 and EARLY + L <= ITERS

    NBATCH = B // P
    LQ = -(-L // QB)
    ST = QR
    TPS = 5
    SW = ST * TPS
    TILES = QUADS
    STORES = TILES // TPS
    SBANKS = 3
    assert TILES == STORES * TPS

    def positions(t):
        return range(t * QB, min(t * QB + QB, L))

    h1_dram = nc.dram_tensor("h1_scratch", (NPAD, D), F32, kind="Internal").ap()
    gm_dram = nc.dram_tensor("gm_scratch", (NPAD, 2 * D), F32, kind="Internal").ap()

    with ExitStack() as ctx:
        def sb(name, shape, dt=F32):
            return ctx.enter_context(nc.sbuf_tensor(name, shape, dt))

        def ps(name):
            return ctx.enter_context(nc.psum_tensor(name, [P, 512], F32))

        def sem(name):
            return ctx.enter_context(nc.semaphore(name))

        def carve(buf):
            at = [0]

            def take(n, parts=P):
                at[0] += n
                assert at[0] <= buf.shape[1]
                return buf[0:parts, at[0] - n:at[0]]
            return take

        accT = sb("accT", [P, NPAD])
        gnat = sb("gnat", [P, NB * D])
        arena = sb("arena", [P, L * 2 * D])
        nhT = sb("nhT", [P, L * P])
        stages = sb("stages", [P, 2 * SW])
        split = accT[:, :].bitcast(F16).rearrange("p (q k n) -> p q k n", k=2, n=QR)
        gnat_b = gnat[:, :].rearrange("p (b d) -> p b d", d=D)
        take = carve(arena)
        gath = take(SETS * Q * D).rearrange("p (s d) -> p s d", d=D)
        sel = take(SETS * Q * W).rearrange("p (s w) -> p s w", w=W)
        rowrel = take(NG * Q)
        val = take(NG * Q)
        col = take(NG * Q).bitcast(I32)
        take = carve(nhT)
        quadT = take(QR)
        hrow = take(QR).rearrange("p (b d) -> p b d", d=D)
        grow = take(QR).rearrange("p (b d) -> p b d", d=D)
        mrow = take(QR).rearrange("p (b d) -> p b d", d=D)
        row_i = take(NG * Q).bitcast(I32)
        iota_i = take(P).bitcast(I32)
        glu_sb = take(2 * D).rearrange("p (w d) -> p w d", w=2)
        pos_sb = take(D, L)
        take = carve(stages)
        item_i, inp_i, ali_i = (take(NBATCH * L).bitcast(I32).rearrange("p (b l) -> p b l", l=L) for _ in range(3))
        item_f, pick, ali_f, cidx_f = (take(NBATCH * L).rearrange("p (b l) -> p b l", l=L) for _ in range(4))
        last_i, span_i = (take(NG, 1).bitcast(I32) for _ in range(2))
        first_f = take(NG, 1)
        ok_f = take(1, 1)
        seqs = [b[:, 0:L * 2 * D].rearrange("p (l c d) -> p l c d", l=L, c=2) for b in (arena, gnat)]

        idx_ring = sb("idx_ring", [P, SETS, Q], I32)
        first_i = sb("first_i", [1, NG], I32)
        nwin_i = sb("nwin_i", [1, NG], I32)
        nmax_i = sb("nmax_i", [1, 1], I32)
        ready_i = sb("ready_i", [1, NG], I32)
        rowm = sb("rowm", [P, Q])
        iota = sb("iota", [P, P])
        ident = sb("ident", [P, P])
        ones = sb("ones", [1, P])
        zero = sb("zero", [P, 1])
        ss = sb("ss", [P, 2, QB])
        nrm = sb("nrm", [P, 2, QB])
        nmx = sb("nmx", [P, 2, QB])
        rn = sb("rn", [P, 2, QB])
        rnw = sb("rnw", [P, QB])
        mask = sb("mask", [P, NBATCH, L])
        cidx = sb("cidx", [P, NBATCH, L], I32)
        cnt = sb("cnt", [P, NBATCH])
        rcnt = sb("rcnt", [P, NBATCH])
        w1_sb = sb("w1_sb", [P, 2, D])
        posT = sb("posT", [P, L])
        pw = sb("pw", [P, L])
        gluT = sb("gluT", [P, 2, D])
        b1 = sb("b1", [P, 1])
        w2_sb = sb("w2_sb", [P, 1])
        hsn, hsT, gb, sess, selrow = (sb(n, [P, P]) for n in ("hsn", "hsT", "gb", "sess", "selrow"))
        part = sb("part", [P, 2, D])
        selT = sb("selT", [P, 2, P], F16)
        beta = sb("beta", [P, L])
        sn = sb("sn", [P, 4])

        win = [ps(f"win{j}") for j in range(SETS)]
        pt = [ps(f"pt{j}") for j in range(2)]
        py = [ps(f"py{j}") for j in range(2)]
        pm = ps("pm")
        first_bc = pm[:, 0:NG]

        loaded = {k: sem("loaded_" + k) for k in ("cols0", "cols", "rows0", "rows", "vals0", "vals", "first",
                                                  "last", "E", "sess", "weights")}
        tail_clear = sem("tail_clear")
        pool_const = sem("pool_const")
        vchain = sem("vchain")
        first_ready = sem("first_ready")
        first_ps = sem("first_ps")
        tables_ready = sem("tables_ready")
        wt_ps = sem("wt_ps")
        wt_sb = sem("wt_sb")
        idx_ready = [sem(f"idx_ready{j}") for j in range(SETS)]
        landed = [sem(f"landed{s}") for s in range(SETS * Q)]
        sel_ready = [sem(f"sel_ready{j}") for j in range(SETS)]
        summed = [sem(f"summed{j}") for j in range(SETS)]
        acc_done = sem("acc_done")
        acc_complete = sem("acc_complete")
        pool_go = sem("pool_go")
        pe_go = sem("pe_go")
        sl_idx = sem("sl_idx")
        sl_landed = [sem(f"sl_landed{k}") for k in range(Q)]
        sl_sel = sem("sl_sel")
        sl_sum = sem("sl_sum")
        sl_group = sem("sl_group")
        n_cp = sem("n_cp")
        n_T = sem("n_T")
        n_ss = sem("n_ss")
        n_root = sem("n_root")
        n_rn = sem("n_rn")
        n_clear = sem("n_clear")
        n_h = sem("n_h")
        n_add = sem("n_add")
        h_stored = sem("h_stored")
        g_stored = sem("g_stored")
        q_ss = sem("q_ss")
        q_root = sem("q_root")
        q_rn = sem("q_rn")
        q_g = sem("q_g")
        q_T = sem("q_T")
        q_cp = sem("q_cp")
        q_high = sem("q_high")
        q_m = sem("q_m")
        q_mrow = sem("q_mrow")
        m_stored = sem("m_stored")
        quad_done = sem("quad_done")
        seq_free = [sem(f"seq_free{k}") for k in range(2)]
        got = [[sem(f"got{k}_{t}") for t in range(LQ)] for k in range(2)]
        s_T = sem("s_T")
        s_nh = sem("s_nh")
        s_hs = sem("s_hs")
        s_hsT = sem("s_hsT")
        s_hsc = sem("s_hsc")
        s_gp = sem("s_gp")
        s_z = sem("s_z")
        s_u = sem("s_u")
        s_sig = sem("s_sig")
        s_beta = sem("s_beta")
        s_sess = sem("s_sess")
        s_sq = sem("s_sq")
        s_sel = sem("s_sel")
        s_selT = sem("s_selT")
        s_selc = sem("s_selc")
        s_tile = sem("s_tile")
        s_copied = [sem(f"s_copied{k}") for k in range(SBANKS)]
        s_out = [sem(f"s_out{k}") for k in range(2)]

        block = ctx.enter_context(nc.Block())

        def used(layer, j):
            return layer * (ITERS + (1 if j == 0 else 0))

        def acc_at(layer, g):
            return SETS + 1 + layer * NG + g

        def rounds(eng, layer, body, setup):
            if layer == 0:
                with eng.Fori(0, EARLY) as i:
                    body(i)
                setup()
                with eng.Fori(EARLY, ITERS) as i:
                    body(i)
                    advance(eng, i)
            else:
                with eng.Fori(0, ITERS) as i:
                    body(i)
                    advance(eng, i)

        steppers = {}

        def start_quads(eng, name, step):
            reg = eng.alloc_register(name + "_quads")
            steppers[name] = (reg, step)
            return name

        def advance(eng, i):
            name = names[eng]
            reg, step = steppers[name]
            ready = eng.value_load(ready_i[0:1, bass.ds(i * SETS + SETS, 1)], min_val=0, max_val=QUADS - 1)
            done = eng.snap(reg, min_val=0, max_val=QUADS - 1)
            with eng.If(ready > done):
                step(done, i * SETS + SETS)
                eng.reg_add(reg, reg, 1)

        def finish_quads(eng):
            reg, step = steppers[names[eng]]
            first = eng.snap(reg, min_val=0, max_val=QUADS - 1)
            with eng.Fori(first, QUADS) as q:
                step(q, None)

        names = {}
        layer_now = [0]

        def quads_of(eng, name, step):
            names[eng] = name
            start_quads(eng, name, lambda q, g: step(layer_now[0], q, g))

        def reset_quads(eng, layer):
            layer_now[0] = layer
            eng.reg_mov(steppers[names[eng]][0], 0)

        def rows_of(dram, q):
            return dram[bass.ds(q * QR, QR), :].rearrange("(b p) d -> p b d", p=P)

        @block.sync
        def _(sp):
            def edges(src, dst, g0, g1, s):
                sp.dma_start(dst[:, g0 * Q:g1 * Q].rearrange("p (g q) -> p g q", q=Q),
                             src[g0 * GE:g1 * GE].rearrange("(g p q) -> p g q", p=P, q=Q)).then_inc(s, 16)

            def short_group(src, dst, s):
                sp.dma_start(dst[0:TP, FULL * Q:NG * Q],
                             src[FULL * GE:NNZ].rearrange("(p q) -> p q", q=Q)).then_inc(s, 16)

            first = adj_row[0:FULL * GE].rearrange("(g n) -> g n", n=GE)
            edges(adj_col, col, 0, EG, loaded["cols0"])
            sp.dma_start(first_i[0:1, 0:FULL], first[:, 0:1].rearrange("g o -> o g"),
                         allow_slow_non_contiguous=True).then_inc(loaded["first"], 16)
            sp.dma_start(first_i[0:1, FULL:NG], adj_row[FULL * GE:FULL * GE + 1].rearrange("(o n) -> o n", o=1)
                         ).then_inc(loaded["first"], 16)
            edges(adj_row, row_i, 0, EG, loaded["rows0"])
            edges(adj_val, val, 0, EG, loaded["vals0"])
            sp.wait_ge(tail_clear, 1)
            for src, dst, k in ((adj_row, row_i, "rows"), (adj_col, col, "cols"), (adj_val, val, "vals")):
                edges(src, dst, EG, FULL, loaded[k])
                short_group(src, dst, loaded[k])
            sp.dma_start(last_i[0:1, 0:FULL], first[:, GE - 1:GE].rearrange("g o -> o g"),
                         allow_slow_non_contiguous=True).then_inc(loaded["last"], 16)
            sp.dma_start(last_i[0:1, FULL:NG], adj_row[NNZ - 1:NNZ].rearrange("(o n) -> o n", o=1)
                         ).then_inc(loaded["last"], 16)
            sp.dma_start(w1_sb[:, :, :], w1.rearrange("(h p) e -> p h e", p=P)).then_inc(loaded["weights"], 16)
            sp.dma_start(pos_sb, pos_emb).then_inc(loaded["weights"], 16)
            sp.dma_start(glu_sb[:, 0, :], glu1_w).then_inc(loaded["weights"], 16)
            sp.dma_start(glu_sb[:, 1, :], glu2_w).then_inc(loaded["weights"], 16)
            sp.dma_start(b1[:, :], glu1_b.rearrange("(p o) -> p o", o=1)).then_inc(loaded["weights"], 16)
            sp.dma_start(w2_sb[:, :], w2).then_inc(loaded["weights"], 16)
            for dst, src in ((item_i, items), (inp_i, inputs), (ali_i, alias)):
                sp.dma_start(dst, src.rearrange("(b p) l -> p b l", p=P)).then_inc(loaded["sess"], 16)
            sp.dma_start(gnat_b[:, 0:FB, :], E[0:FB * P, :].rearrange("(b p) d -> p b d", p=P)
                         ).then_inc(loaded["E"], 16)
            sp.dma_start(gnat_b[0:LASTB, FB, :], E[FB * P:N, :]).then_inc(loaded["E"], 16)

            def store_quad(layer, q, g):
                if layer == 0:
                    sp.wait_ge(n_h, q + 1)
                    sp.dma_start(rows_of(h1_dram, q), hrow).then_inc(h_stored, 16)
                else:
                    sp.wait_ge(n_add, q + (QUADS + 1))
                    sp.dma_start(rows_of(gm_dram, q)[:, :, 0:D], gnat_b[:, bass.ds(q * QB, QB), :]).then_inc(g_stored, 16)
                    sp.wait_ge(q_mrow, q + 1)
                    sp.dma_start(rows_of(gm_dram, q)[:, :, D:2 * D], mrow).then_inc(m_stored, 16)

            quads_of(sp, "sp", store_quad)
            sp.wait_ge(tables_ready, 1)
            for layer in range(LAYERS):
                reset_quads(sp, layer)
                rounds(sp, layer, lambda i: None, lambda: None) if layer else None
                if layer == 0:
                    with sp.Fori(EARLY, ITERS) as i:
                        advance(sp, i)
                finish_quads(sp)

            for n in range(NBATCH * STORES):
                b, m = divmod(n, STORES)
                items_ = min(SW, N - m * SW)
                for s in range(n * TPS, (n + 1) * TPS):
                    sp.wait_ge(s_copied[s % SBANKS], s // SBANKS + 1)
                sp.dma_start(scores[b * P:(b + 1) * P, m * SW:m * SW + items_],
                             stages[:, (n % 2) * SW:(n % 2) * SW + items_]).then_inc(s_out[n % 2], 16)
            for k in range(2):
                sp.wait_ge(s_out[k], 16 * (NBATCH * STORES // 2))

        @block.gpsimd
        def _(pool):
            def gather(dst, src, index, s):
                nc.gpsimd.indirect_dma_start(dst, None, src, bass.IndirectOffsetOnAxis(ap=index, axis=0)
                                             ).then_inc(s, 16)

            def gather_group(table, j, use, parts):
                pool.wait_ge(idx_ready[j], use + 1)
                pool.sem_inc(pool_go, 1)
                for k in range(Q):
                    gather(gath[0:parts, j * Q + k, :], table, idx_ring[0:parts, j, k:k + 1], landed[j * Q + k])

            slow_groups = pool.alloc_register("pool_slow_groups")
            pool.reg_mov(slow_groups, 0)

            def slow_gathers(table):
                most = pool.value_load(nmax_i[0:1, 0:1], min_val=0, max_val=NB)
                with pool.If(most > 0):
                    with pool.Fori(0, NG) as g:
                        windows = pool.value_load(nwin_i[0:1, bass.ds(g, 1)], min_val=0, max_val=NB)
                        with pool.If(windows > 0):
                            m = pool.snap(slow_groups, min_val=0, max_val=2 * NG)
                            pool.wait_ge(sl_group, m + 1)
                            nc.gpsimd.tensor_copy(idx_ring[:, 0, :], col[:, bass.ds(g * Q, Q)]).then_inc(sl_idx, 1)
                            pool.wait_ge(sl_idx, m + 1)
                            pool.sem_inc(pool_go, 1)
                            for k in range(Q):
                                gather(gath[:, k, :], table, idx_ring[:, 0, k:k + 1], sl_landed[k])
                            pool.reg_add(slow_groups, slow_groups, 1)

            nc.gpsimd.iota(iota_i, pattern=[[1, P]], base=0, channel_multiplier=0).then_inc(pool_const, 1)
            nc.gpsimd.memset(ident[:, :], 0.0).then_inc(pool_const, 1)
            pool.wait_ge(pool_const, 2)
            nc.gpsimd.affine_select(out=ident[:, :], in_=ident[:, :], compare_op=ALU.not_equal, fill=1.0,
                                    base=0, pattern=[[-1, P]], channel_multiplier=1).then_inc(pool_const, 1)

            for layer, table in enumerate((E, h1_dram)):
                if layer:
                    pool.wait_ge(h_stored, 16 * (QUADS + 1))
                with pool.Fori(0, ITERS) as i:
                    for j in range(SETS):
                        gather_group(table, j, used(layer, j) + i, P)
                gather_group(table, 0, used(layer, 0) + ITERS, TP)
                pool.wait_ge(tables_ready, 1)
                pool.wait_ge(acc_done, acc_at(layer, NG))
                slow_gathers(table)

            pool.wait_ge(g_stored, 16 * QUADS)
            pool.wait_ge(m_stored, 16 * (QUADS + 1))
            for b in range(NBATCH):
                h = b % 2
                pool.wait_ge(seq_free[h], b // 2 + 1)
                for l in range(L):
                    gather(seqs[h][:, l, :, :].rearrange("p c d -> p (c d)"), gm_dram, cidx[:, b, l:l + 1],
                           got[h][l // QB])

        FIRST_T = 2
        HELD = 12
        SLOTS = LQ - FIRST_T
        bound = [(TILES - HELD) * x // SLOTS for x in range(SLOTS + 1)]

        def tiles_beside(t):
            return range(bound[t - FIRST_T], bound[t - FIRST_T + 1]) if t >= FIRST_T else range(0)

        def tile_items(m):
            return min(ST, N - m * ST)

        @block.tensor
        def _(pe):
            mm, tr = nc.tensor.matmul, nc.tensor.transpose

            def sum_group(j, use, added, parts):
                pe.wait_ge(sel_ready[j], Q * (use + 1))
                pe.wait_ge(acc_done, added - SETS + 1)
                for k in range(Q):
                    s = j * Q + k
                    pe.wait_ge(landed[s], 16 * (use + 1))
                    last = mm(win[j][:, 0:W], gath[0:parts, s, :], sel[0:parts, s, :], start=k == 0, stop=k == Q - 1)
                last.then_inc(summed[j], 1)

            slow_groups = pe.alloc_register("pe_slow_groups")
            slow_windows = pe.alloc_register("pe_slow_windows")
            pe.reg_mov(slow_groups, 0)
            pe.reg_mov(slow_windows, 0)

            def slow_sums(layer):
                pe.wait_ge(acc_done, acc_at(layer, NG))
                most = pe.value_load(nmax_i[0:1, 0:1], min_val=0, max_val=NB)
                with pe.If(most > 0):
                    with pe.Fori(0, NG) as g:
                        windows = pe.value_load(nwin_i[0:1, bass.ds(g, 1)], min_val=0, max_val=NB)
                        with pe.If(windows > 0):
                            m = pe.snap(slow_groups, min_val=0, max_val=2 * NG)
                            for k in range(Q):
                                pe.wait_ge(sl_landed[k], 16 * (m + 1))
                            pe.sem_inc(pe_go, 1)
                            with pe.Fori(0, windows):
                                t = pe.snap(slow_windows, min_val=0, max_val=4 * NG)
                                pe.wait_ge(sl_sel, t + 1)
                                for k in range(Q):
                                    last = mm(win[0][:, 0:W], gath[:, k, :], sel[:, k, :], start=k == 0, stop=k == Q - 1)
                                last.then_inc(sl_sum, 1)
                                pe.reg_add(slow_windows, slow_windows, 1)
                            pe.reg_add(slow_groups, slow_groups, 1)

            def quad_products(layer, q, g):
                pe.wait_ge(n_cp, q + (layer * QUADS + 1))
                for b in range(QB):
                    last = tr(pt[0][:, b * P:(b + 1) * P], quadT[:, b * P:(b + 1) * P], ident[:, :])
                last.then_inc(n_T, 1)
                if layer == LAYERS - 1:
                    pe.wait_ge(q_g, q + 1)
                    for b in range(QB):
                        last = tr(pt[1][:, b * P:(b + 1) * P], grow[:, b, :], ident[:, :])
                    last.then_inc(q_T, 1)
                    pe.wait_ge(q_cp, q + 1)
                    for b in range(QB):
                        last = mm(py[1][:, b * D:(b + 1) * D], quadT[:, b * P:(b + 1) * P], w1_sb[:, 1, :],
                                  start=True, stop=True)
                    last.then_inc(q_m, 1)

            def weights():
                pe.wait_ge(pool_const, 3)
                pe.wait_ge(loaded["weights"], 16 * 6)
                tr(pt[1][:, 0:L], pos_sb, ident[0:L, 0:L])
                for w in range(2):
                    last = tr(pt[1][:, (w + 1) * P:(w + 2) * P], glu_sb[:, w, :], ident[:, :])
                last.then_inc(wt_ps, 1)
                pe.wait_ge(wt_sb, 1)
                mm(pt[1][:, 3 * P:3 * P + L], w1_sb[:, 0, :], posT[:, :], start=True, stop=True).then_inc(wt_ps, 1)
                pe.wait_ge(tables_ready, 1)

            pe.wait_ge(first_ready, 1)
            mm(first_bc, ones[:, :], first_f, start=True, stop=True).then_inc(first_ps, 1)
            quads_of(pe, "pe", quad_products)
            for layer in range(LAYERS):
                reset_quads(pe, layer)

                def sums(i):
                    for j in range(SETS):
                        sum_group(j, used(layer, j) + i, i * SETS + (acc_at(layer, 0) + j), P)

                rounds(pe, layer, sums, weights)
                sum_group(0, used(layer, 0) + ITERS, acc_at(layer, FULL), TP)
                slow_sums(layer)
                finish_quads(pe)

            def batch_quad(b, t):
                c = b * LQ + t
                pe.wait_ge(got[b % 2][t], 16 * len(positions(t)) * (b // 2 + 1))
                if c >= 2:
                    pe.wait_ge(s_nh, c - 1)
                for x, l in enumerate(positions(t)):
                    last = tr(pt[c % 2][:, x * P:(x + 1) * P], seqs[b % 2][:, l, 1, :], ident[:, :])
                last.then_inc(s_T, 1)

            def glu_quad(b, t):
                c = b * LQ + t
                n = len(positions(t))
                pe.wait_ge(s_nh, c + 1)
                if c >= 2:
                    pe.wait_ge(s_u, c - 1)
                mm(py[c % 2][:, 0:n * P], gluT[:, 0, :], nhT[:, t * QR:t * QR + n * P], start=True, stop=True
                   ).then_inc(s_z, 1)

            def batch_weights(b):
                for t in range(2):
                    glu_quad(b, t)
                pe.wait_ge(s_hs, b + 1)
                tr(pm[:, 0:P], hsn[:, :], ident[:, :]).then_inc(s_hsT, 1)
                pe.wait_ge(s_hsc, b + 1)
                mm(pm[:, P:2 * P], gluT[:, 1, :], hsT[:, :], start=True, stop=True).then_inc(s_gp, 1)
                for t in range(LQ):
                    if t + 2 < LQ:
                        glu_quad(b, t + 2)
                    pe.wait_ge(s_sig, b * LQ + t + 1)
                    for l in positions(t):
                        last = mm(pm[:, 2 * P + l:2 * P + l + 1], nhT[:, l * P:(l + 1) * P], w2_sb[:, :],
                                  start=True, stop=True)
                last.then_inc(s_beta, 1)

            def select_T(b):
                pe.wait_ge(s_sel, b + 1)
                tr(pm[:, 3 * P:4 * P], selrow[:, :], ident[:, :]).then_inc(s_selT, 1)

            def score_tile(b, m):
                s = b * TILES + m
                n = tile_items(m)
                pe.wait_ge(s_selc, b + 1)
                if s >= SBANKS:
                    pe.wait_ge(s_copied[s % SBANKS], s // SBANKS)
                out = win[s % SBANKS][:, 0:n]
                mm(out, selT[:, 0, :], split[:, m, 0, 0:n], start=True, stop=False)
                mm(out, selT[:, 0, :], split[:, m, 1, 0:n], start=False, stop=False)
                mm(out, selT[:, 1, :], split[:, m, 0, 0:n], start=False, stop=True).then_inc(s_tile, 1)

            pe.wait_ge(quad_done, 2 * QUADS + 1)
            for b in range(NBATCH):
                for t in range(LQ):
                    batch_quad(b, t)
                    if b and t == FIRST_T - 1:
                        select_T(b - 1)
                    if b:
                        for m in tiles_beside(t):
                            score_tile(b - 1, m)
                batch_weights(b)
                if b:
                    for m in range(TILES - HELD, TILES):
                        score_tile(b - 1, m)
            select_T(NBATCH - 1)
            for m in range(TILES):
                score_tile(NBATCH - 1, m)

        def copy_tile(eng, b, m):
            s = b * TILES + m
            n = s // TPS
            eng.wait_ge(s_tile, s + 1)
            if n >= 2:
                eng.wait_ge(s_out[n % 2], 16 * (n // 2))
            at = (n % 2) * SW + (s % TPS) * ST
            out, bank = stages[:, at:at + tile_items(m)], win[s % SBANKS][:, 0:tile_items(m)]
            unscale = 1.0 / (ITEM_SCALE * SELECT_SCALE)
            if eng is dve_engine[0]:
                nc.vector.tensor_scalar(out, bank, unscale, None, ALU.mult).then_inc(s_copied[s % SBANKS], 1)
            else:
                nc.scalar.mul(out, bank, unscale).then_inc(s_copied[s % SBANKS], 1)

        dve_engine = [None]

        @block.scalar
        def _(act):
            def columns(j, use, g):
                act.wait_ge(summed[j], use + 1)
                nc.scalar.copy(idx_ring[:, j, :], col[:, bass.ds(g * Q, Q)]).then_inc(idx_ready[j], 1)

            def quad_norms(layer, q, g):
                v = q + layer * QUADS
                if g is None:
                    act.wait_ge(acc_complete, layer + 1)
                else:
                    act.wait_ge(acc_done, g + acc_at(layer, 0))
                act.wait_ge(quad_done, v + 1)
                nc.scalar.copy(quadT, accT[:, bass.ds(q * QR, QR)]).then_inc(n_cp, 1)
                act.wait_ge(n_T, v + 1)
                for b in range(QB):
                    nc.scalar.activation(py[0][:, b * D:(b + 1) * D], pt[0][:, b * D:(b + 1) * D], ACT.Square,
                                         accum_out=ss[:, 0, b:b + 1]).then_inc(n_ss, 1)
                act.wait_ge(n_ss, v * QB + QB)
                nc.scalar.activation(nrm[:, 0, :], ss[:, 0, :], ACT.Sqrt).then_inc(n_root, 1)
                if layer == LAYERS - 1:
                    act.wait_ge(n_add, v + 1)
                    for b in range(QB):
                        nc.scalar.activation(py[0][:, b * D:(b + 1) * D], gnat[:, bass.ds(q * QR + b * D, D)], ACT.Square,
                                             accum_out=ss[:, 1, b:b + 1]).then_inc(q_ss, 1)
                    act.wait_ge(q_ss, q * QB + QB)
                    nc.scalar.activation(nrm[:, 1, :], ss[:, 1, :], ACT.Sqrt).then_inc(q_root, 1)
                    act.wait_ge(q_T, q + 1)
                    nc.scalar.copy(quadT, pt[1][:, :]).then_inc(q_cp, 1)

            quads_of(act, "act", quad_norms)
            act.wait_ge(loaded["cols0"], 16)
            for layer in range(LAYERS):
                reset_quads(act, layer)

                def all_columns(i):
                    for j in range(SETS):
                        columns(j, used(layer, j) + i, i * SETS + j)

                start = 0
                all_columns(0)
                if layer == 0:
                    with act.Fori(0, EARLY - 1) as i:
                        all_columns(i + 1)
                    act.wait_ge(loaded["cols"], 32)
                    all_columns(EARLY)
                    act.wait_ge(tables_ready, 1)
                    start = EARLY
                with act.Fori(start, ITERS - 1) as i:
                    all_columns(i + 1)
                    advance(act, i)
                columns(0, used(layer, 0) + ITERS, FULL)
                advance(act, ITERS - 1)
                finish_quads(act)

            def tanh_quad(b, t):
                c = b * LQ + t
                if b and t == 0:
                    act.wait_ge(s_beta, b)
                act.wait_ge(s_T, c + 1)
                for x, l in enumerate(positions(t)):
                    last = nc.scalar.activation(nhT[:, l * P:(l + 1) * P], pt[c % 2][:, x * P:(x + 1) * P],
                                                ACT.Tanh, bias=pw[:, L - 1 - l:L - l])
                last.then_inc(s_nh, 1)

            act.wait_ge(quad_done, 2 * QUADS + 1)
            act.wait_ge(m_stored, 16 * (QUADS + 1))
            for b in range(NBATCH):
                for t in range(LQ):
                    tanh_quad(b, t)
                    if b:
                        for m in tiles_beside(t):
                            copy_tile(act, b - 1, m)
                for t in range(LQ):
                    quad = nhT[:, t * QR:t * QR + len(positions(t)) * P]
                    act.wait_ge(s_u, b * LQ + t + 1)
                    nc.scalar.activation(quad, quad, ACT.Sigmoid).then_inc(s_sig, 1)
                if b:
                    for m in range(TILES - HELD, TILES):
                        copy_tile(act, b - 1, m)
                act.wait_ge(s_sess, b + 1)
                nc.scalar.activation(selrow[:, :], sess[:, :], ACT.Square, accum_out=sn[:, 0:1]).then_inc(s_sq, 1)
                act.wait_ge(s_sq, 2 * b + 1)
                nc.scalar.activation(sn[:, 1:2], sn[:, 0:1], ACT.Sqrt).then_inc(s_sq, 1)
            for m in range(0, TILES, 2):
                copy_tile(act, NBATCH - 1, m)

        @block.vector
        def _(dve):
            v = nc.vector
            dve_engine[0] = dve
            steps = [0]

            def mark(ins):
                steps[0] += 1
                ins.then_inc(vchain, 1)

            def link(ins):
                mark(ins)
                dve.wait_ge(vchain, steps[0])

            mark(v.memset(col[:, FULL * Q:NG * Q], 0))
            mark(v.memset(val[:, FULL * Q:NG * Q], 0.0))
            mark(v.memset(rowrel[:, FULL * Q:NG * Q], -1.0))
            mark(v.memset(ones[:, :], 1.0))
            mark(v.memset(zero[:, :], 0.0))
            link(v.memset(gnat_b[:, FB:NB, :], 0.0))
            dve.sem_inc(tail_clear, 1)
            for j in range(SETS):
                dve.sem_inc(summed[j], 1)
            dve.sem_inc(acc_done, SETS)
            for s in (sl_group, quad_done, seq_free[0], seq_free[1]):
                dve.sem_inc(s, 1)
            for s in (h_stored, m_stored):
                dve.sem_inc(s, 16)
            v.memset(accT[:, :], 0.0).then_inc(acc_done, 1)
            dve.wait_ge(pool_const, 1)
            mark(v.tensor_copy(iota[:, :], iota_i))
            dve.wait_ge(loaded["first"], 32)
            link(v.tensor_copy(first_f, first_i[:, :]))
            dve.sem_inc(first_ready, 1)

            def relative_rows(g0, g1):
                mark(v.tensor_tensor(rowrel[:, g0 * Q:g1 * Q].rearrange("p (g q) -> p g q", q=Q),
                                     row_i[:, g0 * Q:g1 * Q].rearrange("p (g q) -> p g q", q=Q),
                                     first_bc[:, g0:g1].unsqueeze(2).broadcast_to([P, g1 - g0, Q]), ALU.subtract))

            dve.wait_ge(first_ps, 1)
            dve.wait_ge(loaded["rows0"], 16)
            relative_rows(0, EG)
            dve.wait_ge(vchain, steps[0])
            dve.wait_ge(loaded["vals0"], 16)

            def late():
                dve.wait_ge(loaded["rows"], 32)
                relative_rows(EG, FULL)
                link(v.tensor_tensor(rowrel[0:TP, FULL * Q:NG * Q], row_i[0:TP, FULL * Q:NG * Q],
                                     first_bc[0:TP, FULL:NG].broadcast_to([TP, Q]), ALU.subtract))
                dve.wait_ge(loaded["last"], 32)
                link(v.tensor_tensor(span_i, last_i, first_i[:, :], ALU.subtract))
                link(v.tensor_scalar(nwin_i[:, :], span_i, W.bit_length() - 1, None, ALU.arith_shift_right))
                link(v.tensor_reduce(nmax_i[:, :], nwin_i[:, :], AX.X, ALU.max))
                mark(v.tensor_scalar(ok_f, nmax_i[:, :], 0.0, None, ALU.is_equal))
                link(v.tensor_scalar(span_i, first_i[:, :], QR.bit_length() - 1, None, ALU.arith_shift_right))
                link(v.tensor_scalar(ready_i[:, :], span_i, ok_f, None, ALU.mult))
                dve.sem_inc(tables_ready, 1)
                dve.wait_ge(loaded["vals"], 32)

            def weights_and_sessions():
                dve.wait_ge(wt_ps, 1)
                mark(v.tensor_copy(posT[:, :], pt[1][:, 0:L]))
                link(v.tensor_copy(gluT[:, :, :], pt[1][:, P:3 * P].rearrange("p (w f) -> p w f", w=2)))
                dve.sem_inc(wt_sb, 1)
                dve.wait_ge(wt_ps, 2)
                link(v.tensor_copy(pw[:, :], pt[1][:, 3 * P:3 * P + L]))
                dve.wait_ge(loaded["sess"], 48)
                mark(v.memset(cidx_f, 0.0))
                mark(v.tensor_copy(item_f, item_i))
                mark(v.tensor_copy(ali_f, ali_i))
                link(v.tensor_scalar(mask[:, :, :], inp_i, 0.0, None, ALU.not_equal))
                mark(v.tensor_reduce(cnt[:, :], mask[:, :, :], AX.X, ALU.add))
                link(v.tensor_scalar(pick, item_f, 0.0, float(N), ALU.is_lt, ALU.mult))
                mark(v.reciprocal(rcnt[:, :], cnt[:, :]))
                link(v.tensor_tensor(item_f, item_f, pick, ALU.add))
                link(v.tensor_scalar(item_f, item_f, 0.0, float(N - 1), ALU.max, ALU.min))

            def select_group(j, use, g):
                dve.wait_ge(summed[j], use + 1)
                for k in range(Q):
                    v.tensor_scalar(sel[:, j * Q + k, :], iota[:, :], rowrel[:, bass.ds(g * Q + k, 1)],
                                    val[:, bass.ds(g * Q + k, 1)], ALU.is_equal, ALU.mult).then_inc(sel_ready[j], 1)

            def add_group(layer, j, use, g):
                row0 = dve.value_load(first_i[0:1, bass.ds(g, 1)], min_val=0, max_val=N - 1)
                dve.wait_ge(summed[j], use + 2)
                dve.wait_ge(acc_done, acc_at(layer, 0) + g)
                dst = accT[:, bass.ds(row0, W)]
                v.tensor_tensor(dst, dst, win[j][:, 0:W], ALU.add).then_inc(acc_done, 1)

            def adds(layer, i):
                for j in range(SETS):
                    nj, more = (j + 1) % SETS, (j + 1) // SETS
                    select_group(nj, used(layer, nj) + i + more, i * SETS + j + 1)
                    add_group(layer, j, used(layer, j) + i, i * SETS + j)

            slow_windows = dve.alloc_register("dve_slow_windows")
            dve.reg_mov(slow_windows, 0)
            place = dve.alloc_register("dve_window_row")

            def slow_adds():
                most = dve.value_load(nmax_i[0:1, 0:1], min_val=0, max_val=NB)
                with dve.If(most > 0):
                    with dve.Fori(0, NG) as g:
                        windows = dve.value_load(nwin_i[0:1, bass.ds(g, 1)], min_val=0, max_val=NB)
                        with dve.If(windows > 0):
                            row0 = dve.value_load(first_i[0:1, bass.ds(g, 1)], min_val=0, max_val=N - 1)
                            v.tensor_copy(rowm[:, :], rowrel[:, bass.ds(g * Q, Q)])
                            dve.drain()
                            dve.reg_mov(place, row0)
                            with dve.Fori(0, windows):
                                v.tensor_scalar(rowm[:, :], rowm[:, :], float(W), None, ALU.subtract)
                                dve.drain()
                                for k in range(Q):
                                    v.tensor_scalar(sel[:, k, :], iota[:, :], rowm[:, k:k + 1],
                                                    val[:, bass.ds(g * Q + k, 1)], ALU.is_equal, ALU.mult)
                                dve.drain()
                                dve.sem_inc(sl_sel, 1)
                                t = dve.snap(slow_windows, min_val=0, max_val=4 * NG)
                                dve.wait_ge(sl_sum, t + 1)
                                dve.reg_add(place, place, W)
                                dst = accT[:, bass.ds(dve.snap(place, min_val=W, max_val=N - 1), W)]
                                v.tensor_tensor(dst, dst, win[0][:, 0:W], ALU.add)
                                dve.drain()
                                dve.reg_add(slow_windows, slow_windows, 1)
                            dve.sem_inc(sl_group, 1)

            def over(x, n=QB):
                return x.unsqueeze(2).broadcast_to([P, n, D])

            def quad_rows(layer, q, g):
                w = q + layer * QUADS
                weight = 1.0 if layer < LAYERS - 1 else 1.0 / (LAYERS + 1)
                dve.wait_ge(n_cp, w + 1)
                if layer < LAYERS - 1:
                    v.tensor_copy(accT[:, bass.ds(q * QR, QR)], zero[:, :].broadcast_to([P, QR])).then_inc(n_clear, 1)
                    dve.wait_ge(n_clear, w + 1)
                dve.wait_ge(n_root, w + 1)
                v.tensor_scalar(nmx[:, 0, :], nrm[:, 0, :], EPS, None, ALU.max).then_inc(n_rn, 1)
                dve.wait_ge(n_rn, w * 3 + 1)
                v.reciprocal(rn[:, 0, :], nmx[:, 0, :]).then_inc(n_rn, 1)
                dve.wait_ge(n_rn, w * 3 + 2)
                v.tensor_scalar(rnw[:, :], rn[:, 0, :], weight, None, ALU.mult).then_inc(n_rn, 1)
                dve.wait_ge(n_rn, w * 3 + 3)
                if layer == 0:
                    dve.wait_ge(h_stored, w * 16 + 16)
                v.tensor_tensor(hrow, pt[0][:, :].rearrange("p (b d) -> p b d", d=D), over(rnw[:, :]), ALU.mult
                                ).then_inc(n_h, 1)
                dve.wait_ge(n_h, w + 1)
                here = gnat_b[:, bass.ds(q * QB, QB), :]
                v.scalar_tensor_tensor(here, here, weight, hrow, ALU.mult, ALU.add).then_inc(n_add, 1)
                dve.wait_ge(n_add, w + 1)
                if layer == LAYERS - 1:
                    dve.wait_ge(q_root, q + 1)
                    v.tensor_scalar(nmx[:, 1, :], nrm[:, 1, :], EPS, None, ALU.max).then_inc(q_rn, 1)
                    dve.wait_ge(q_rn, q * 2 + 1)
                    v.reciprocal(rn[:, 1, :], nmx[:, 1, :]).then_inc(q_rn, 1)
                    dve.wait_ge(q_rn, q * 2 + 2)
                    v.tensor_tensor(grow, here, over(rn[:, 1, :]), ALU.mult).then_inc(q_g, 1)
                    dve.wait_ge(q_cp, q + 1)
                    high, low = (accT[:, bass.ds(q * QR + x * (QR // 2), QR // 2)].bitcast(F16) for x in range(2))
                    v.tensor_scalar(high, quadT, ITEM_SCALE, None, ALU.mult).then_inc(q_high, 1)
                    dve.wait_ge(q_high, q + 1)
                    v.scalar_tensor_tensor(low, quadT, ITEM_SCALE, high, ALU.mult, ALU.subtract)
                    dve.wait_ge(q_m, q + 1)
                    dve.wait_ge(m_stored, q * 16 + 16)
                    v.tensor_tensor(mrow, py[1][:, :].rearrange("p (b d) -> p b d", d=D), over(nmx[:, 1, :]), ALU.mult
                                    ).then_inc(q_mrow, 1)
                    dve.wait_ge(q_mrow, q + 1)
                dve.sem_inc(quad_done, 1)

            quads_of(dve, "dve", quad_rows)
            for layer in range(LAYERS):
                reset_quads(dve, layer)

                select_group(0, used(layer, 0), 0)
                if layer == 0:
                    with dve.Fori(0, EARLY) as i:
                        adds(layer, i)
                    late()
                    weights_and_sessions()
                    dve.wait_ge(loaded["E"], 32)
                    c0 = steps[0]
                    with dve.Fori(EARLY, EARLY + L) as i:
                        adds(layer, i)
                        here = item_f[:, :, bass.ds(i - EARLY, 1)].broadcast_to([P, NBATCH, L])
                        v.scalar_tensor_tensor(pick, ali_f, 0.0, here, ALU.is_equal, ALU.mult).then_inc(vchain, 1)
                        dve.wait_ge(vchain, i * 3 + (c0 + 1 - 3 * EARLY))
                        v.tensor_tensor(cidx_f, cidx_f, pick, ALU.add).then_inc(vchain, 1)
                        v.tensor_scalar(ali_f, ali_f, -1.0, None, ALU.add).then_inc(vchain, 1)
                        dve.wait_ge(vchain, i * 3 + (c0 + 3 - 3 * EARLY))
                        advance(dve, i)
                    steps[0] += 3 * L
                    link(v.tensor_copy(cidx[:, :, :], cidx_f))
                    with dve.Fori(EARLY + L, ITERS) as i:
                        adds(layer, i)
                        advance(dve, i)
                else:
                    with dve.Fori(0, ITERS) as i:
                        adds(layer, i)
                        advance(dve, i)
                add_group(layer, 0, used(layer, 0) + ITERS, FULL)
                dve.wait_ge(acc_done, acc_at(layer, NG))
                slow_adds()
                dve.drain()
                dve.sem_inc(acc_complete, 1)
                finish_quads(dve)

            def session_sum(b, weight_of, positions_):
                for l in positions_:
                    row, dst = seqs[b % 2][:, l, 0, :], part[:, l % 2, :]
                    if l >= 2:
                        dve.wait_ge(vchain, steps[0] - 1)
                        mark(v.scalar_tensor_tensor(dst, row, weight_of(l), dst, ALU.mult, ALU.add))
                    else:
                        mark(v.tensor_scalar(dst, row, weight_of(l), None, ALU.mult))

            dve.drain()
            for b in range(NBATCH):
                for t in range(LQ):
                    dve.wait_ge(got[b % 2][t], 16 * len(positions(t)) * (b // 2 + 1))
                    session_sum(b, lambda l: mask[:, b, l:l + 1], positions(t))
                dve.wait_ge(vchain, steps[0])
                link(v.tensor_tensor(hsn[:, :], part[:, 0, :], part[:, 1, :], ALU.add))
                v.tensor_scalar(hsn[:, :], hsn[:, :], rcnt[:, b:b + 1], None, ALU.mult).then_inc(s_hs, 1)
                dve.wait_ge(s_hsT, b + 1)
                v.tensor_copy(hsT[:, :], pm[:, 0:P]).then_inc(s_hsc, 1)
                dve.wait_ge(s_gp, b + 1)
                link(v.tensor_scalar(gb[:, :], pm[:, P:2 * P], b1[:, 0:1], None, ALU.add))
                for t in range(LQ):
                    c = b * LQ + t
                    n = len(positions(t))
                    dve.wait_ge(s_z, c + 1)
                    v.tensor_tensor(nhT[:, t * QR:t * QR + n * P].rearrange("p (x b) -> p x b", x=n),
                                    py[c % 2][:, 0:n * P].rearrange("p (x b) -> p x b", x=n),
                                    gb[:, :].unsqueeze(1).broadcast_to([P, n, P]), ALU.add).then_inc(s_u, 1)
                dve.wait_ge(s_beta, b + 1)
                link(v.tensor_tensor(beta[:, :], pm[:, 2 * P:2 * P + L], mask[:, b, :], ALU.mult))
                session_sum(b, lambda l: beta[:, l:l + 1], range(L))
                dve.wait_ge(vchain, steps[0])
                link(v.tensor_tensor(sess[:, :], part[:, 0, :], part[:, 1, :], ALU.add))
                dve.sem_inc(s_sess, 1)
                dve.sem_inc(seq_free[b % 2], 1)
                dve.wait_ge(s_sq, 2 * b + 2)
                link(v.tensor_scalar(sn[:, 2:3], sn[:, 1:2], EPS, None, ALU.max))
                link(v.reciprocal(sn[:, 3:4], sn[:, 2:3]))
                v.tensor_scalar(selrow[:, :], sess[:, :], sn[:, 3:4], W_K * SELECT_SCALE, ALU.mult, ALU.mult).then_inc(s_sel, 1)
                dve.wait_ge(s_selT, b + 1)
                if b:
                    dve.wait_ge(s_tile, b * TILES)
                link(v.tensor_copy(selT[:, 0, :], pm[:, 3 * P:4 * P]))
                v.tensor_tensor(selT[:, 1, :], pm[:, 3 * P:4 * P], selT[:, 0, :], ALU.subtract).then_inc(s_selc, 1)
            for m in range(1, TILES, 2):
                copy_tile(dve, NBATCH - 1, m)


_INS = ["r_items", "r_inputs", "r_alias_inputs", "L0_rec_adj_row", "L0_rec_adj_col", "L0_rec_adj_val",
        "L0_rec_E", "L0_rec_pos_emb", "L0_rec_w1", "L0_rec_w2", "L0_rec_glu1_w", "L0_rec_glu1_b", "L0_rec_glu2_w"]


def kernel(**inputs):
    import numpy as np
    import concourse.bacc as bacc
    from concourse.bass_utils import run_bass_kernel_spmd

    nc = bacc.Bacc("TRN2", target_bir_lowering=False, num_devices=1)
    arrays, args = {}, []
    for name in _INS:
        a = np.ascontiguousarray(inputs[name])
        arrays[f"in_{name}"] = a
        args.append(nc.dram_tensor(f"in_{name}", a.shape, mybir.dt.from_np(a.dtype), kind="ExternalInput").ap())
    shape = (inputs["r_items"].shape[0], inputs["L0_rec_E"].shape[0])
    scores = nc.dram_tensor("scores", shape, F32, kind="ExternalOutput").ap()
    session_graph_scores(nc, *args, scores)
    r = run_bass_kernel_spmd(nc, [arrays], core_ids=[0])
    return r.results[0]["scores"]
```

```python
import concourse.bass as bass
from concourse import mybir
from concourse.alu_op_type import AluOpType as ALU
from contextlib import ExitStack

F32, I32, F16 = mybir.dt.float32, mybir.dt.int32, mybir.dt.float16
ACT = mybir.ActivationFunctionType
AX = mybir.AxisListType

LAYERS = 2
W_K = 12.0
EPS = 1e-12
ITEM_SCALE = 2.0 ** 12
SELECT_SCALE = 2.0 ** 10


def session_graph_scores(nc, items, inputs, alias, adj_row, adj_col, adj_val, E, pos_emb,
                         w1, w2, glu1_w, glu1_b, glu2_w, scores):
    P = 128
    N, D = E.shape
    B, L = items.shape
    NNZ = adj_row.shape[0]
    assert D == P and B % P == 0

    Q = 8
    GE = P * Q
    FULL = NNZ // GE
    TAIL = NNZ - FULL * GE
    TQ = next(q for q in range(1, Q + 1) if TAIL % q == 0 and TAIL // q <= P)
    TP = TAIL // TQ
    NG = FULL + 1
    SETS = 3
    ITERS = FULL // SETS
    EARLY = 6
    EG = EARLY * SETS + 1
    PIECES = EARLY - 1
    assert TAIL > 0 and FULL % SETS == 0
    W = P
    QB = 4
    QR = QB * P
    QUADS = -(-N // QR)
    NB = QUADS * QB
    QB_LAST = -(-(N - (QUADS - 1) * QR) // P)
    NPAD = NB * P
    NROWS = (QUADS - 1) * QR + QB_LAST * P
    FB = N // P
    LASTB = N - FB * P
    assert LAYERS == 2 and EARLY + L <= ITERS

    NBATCH = B // P
    LQ = -(-L // QB)
    ST = QR
    TPS = 3
    NSTAGE = 4
    SW = ST * TPS
    TILES = QUADS
    STORES = -(-TILES // TPS)
    LAST = NBATCH - 1

    def positions(t):
        return range(t * QB, min(t * QB + QB, L))

    h1_dram = nc.dram_tensor("h1_scratch", (NROWS, D), F32, kind="Internal").ap()
    gm_dram = nc.dram_tensor("gm_scratch", (NROWS, 2 * D), F32, kind="Internal").ap()

    with ExitStack() as ctx:
        def sb(name, shape, dt=F32):
            return ctx.enter_context(nc.sbuf_tensor(name, shape, dt))

        def ps(name):
            return ctx.enter_context(nc.psum_tensor(name, [P, 512], F32))

        def sem(name):
            return ctx.enter_context(nc.semaphore(name))

        def carve(buf):
            at = [0]

            def take(n, parts=P):
                at[0] += n
                assert at[0] <= buf.shape[1]
                return buf[0:parts, at[0] - n:at[0]]
            return take

        accT = sb("accT", [P, NPAD])
        gnat = sb("gnat", [P, NB * D])
        arena = sb("arena", [P, L * 2 * D])
        temps = sb("temps", [P, 4 * QR + NG * Q + 2 * P + 2 * D])
        stages = sb("stages", [P, NSTAGE * SW])
        split = accT[:, :].bitcast(F16).rearrange("p (q k n) -> p q k n", k=2, n=QR)
        gnat_b = gnat[:, :].rearrange("p (b d) -> p b d", d=D)
        take = carve(arena)
        gath = take(SETS * Q * D).rearrange("p (s d) -> p s d", d=D)
        sel = take(SETS * Q * W).rearrange("p (s w) -> p s w", w=W)
        rowrel = take(NG * Q)
        val = take(NG * Q)
        col = take(NG * Q).bitcast(I32)
        take = carve(temps)
        quadT = take(QR)
        hrow = take(QR).rearrange("p (b d) -> p b d", d=D)
        grow = take(QR).rearrange("p (b d) -> p b d", d=D)
        mrow = take(QR).rearrange("p (b d) -> p b d", d=D)
        row_i = take(NG * Q).bitcast(I32)
        iota_i = take(P).bitcast(I32)
        glu_sb = take(2 * D).rearrange("p (w d) -> p w d", w=2)
        pos_sb = take(D, L)
        take = carve(stages)
        item_i, inp_i, ali_i = (take(NBATCH * L).bitcast(I32).rearrange("p (b l) -> p b l", l=L) for _ in range(3))
        item_f, pick, ali_f, cidx_f = (take(NBATCH * L).rearrange("p (b l) -> p b l", l=L) for _ in range(4))
        last_i, span_i = (take(NG, 1).bitcast(I32) for _ in range(2))
        first_f = take(NG, 1)
        ok_f = take(1, 1)
        seqs = [b[:, 0:L * 2 * D].rearrange("p (l c d) -> p l c d", l=L, c=2) for b in (arena, gnat)]

        idx_ring = sb("idx_ring", [P, SETS, Q], I32)
        first_i = sb("first_i", [1, NG], I32)
        nwin_i = sb("nwin_i", [1, NG], I32)
        nmax_i = sb("nmax_i", [1, 1], I32)
        ready_i = sb("ready_i", [1, NG], I32)
        rowm = sb("rowm", [P, Q])
        iota = sb("iota", [P, P])
        ident = sb("ident", [P, P])
        ones = sb("ones", [1, P])
        zero = sb("zero", [P, 1])
        ss = sb("ss", [P, 2, QB])
        nrm = sb("nrm", [P, 2, QB])
        nmx = sb("nmx", [P, 2, QB])
        rn = sb("rn", [P, 2, QB])
        mask = sb("mask", [P, NBATCH, L])
        cidx = sb("cidx", [P, NBATCH, L], I32)
        cnt = sb("cnt", [P, NBATCH])
        rcnt = sb("rcnt", [P, NBATCH])
        w1_sb = sb("w1_sb", [P, 2, D])
        posT = sb("posT", [P, L])
        pw = sb("pw", [P, L])
        gluT = sb("gluT", [P, 2, D])
        b1 = sb("b1", [P, 1])
        w2_sb = sb("w2_sb", [P, 1])
        hsn, hsT, gb, sess, selrow = (sb(n, [P, P]) for n in ("hsn", "hsT", "gb", "sess", "selrow"))
        hs_part = sb("hs_part", [P, 2, D])
        sess_part = sb("sess_part", [P, 2, D])
        selT = sb("selT", [P, 2, P], F16)
        beta = sb("beta", [P, L])
        sn = sb("sn", [P, 4])

        win = [ps(f"win{j}") for j in range(SETS)]
        pt = [ps(f"pt{j}") for j in range(2)]
        py = [ps(f"py{j}") for j in range(2)]
        pm = ps("pm")
        first_bc = pm[:, 0:NG]
        beta_banks = (win[2], pm)
        tile_banks = [(win[0], win[1])] * (NBATCH - 1) + [(win[0], win[1], win[2], py[0])]

        loaded = {k: sem("loaded_" + k) for k in ("cols0", "cols", "rows0", "rows", "vals0", "vals", "first",
                                                  "last", "E", "sess", "weights")}
        tail_clear = sem("tail_clear")
        pool_const = sem("pool_const")
        vchain = sem("vchain")
        first_ready = sem("first_ready")
        first_ps = sem("first_ps")
        tables_ready = sem("tables_ready")
        wt_ps = sem("wt_ps")
        wt_sb = sem("wt_sb")
        idx_ready = [sem(f"idx_ready{j}") for j in range(SETS)]
        landed = [sem(f"landed{s}") for s in range(SETS * Q)]
        sel_ready = [sem(f"sel_ready{j}") for j in range(SETS)]
        summed = [sem(f"summed{j}") for j in range(SETS)]
        acc_done = sem("acc_done")
        acc_complete = sem("acc_complete")
        pool_go = sem("pool_go")
        pe_go = sem("pe_go")
        sl_idx = sem("sl_idx")
        sl_landed = [sem(f"sl_landed{k}") for k in range(Q)]
        sl_sel = sem("sl_sel")
        sl_sum = sem("sl_sum")
        sl_group = sem("sl_group")
        n_cp = sem("n_cp")
        n_T = sem("n_T")
        n_ss = sem("n_ss")
        n_root = sem("n_root")
        n_rn = sem("n_rn")
        n_clear = sem("n_clear")
        n_h = sem("n_h")
        n_add = sem("n_add")
        h_stored = sem("h_stored")
        g_stored = sem("g_stored")
        q_ss = sem("q_ss")
        q_root = sem("q_root")
        q_rn = sem("q_rn")
        q_g = sem("q_g")
        q_T = sem("q_T")
        q_gT = sem("q_gT")
        q_cp = sem("q_cp")
        q_split = sem("q_split")
        q_m = sem("q_m")
        q_mrow = sem("q_mrow")
        m_stored = sem("m_stored")
        quad_done = sem("quad_done")
        seq_free = [sem(f"seq_free{k}") for k in range(2)]
        got = [[sem(f"got{k}_{t}") for t in range(LQ)] for k in range(2)]
        s_T = sem("s_T")
        s_nh = sem("s_nh")
        s_hs = sem("s_hs")
        s_hsT = sem("s_hsT")
        s_hsc = sem("s_hsc")
        s_gp = sem("s_gp")
        s_z = sem("s_z")
        s_u = sem("s_u")
        s_sig = sem("s_sig")
        s_beta = sem("s_beta")
        s_beta_read = sem("s_beta_read")
        s_sess = sem("s_sess")
        s_sq = sem("s_sq")
        s_sel = sem("s_sel")
        s_selT = sem("s_selT")
        s_selc = sem("s_selc")
        s_tile = sem("s_tile")
        s_copied = [sem(f"s_copied_by_{k}") for k in ("act", "dve")]
        s_out = [sem(f"s_out{k}") for k in range(NSTAGE)]
        s_out_last = sem("s_out_last")

        block = ctx.enter_context(nc.Block())

        def used(layer, j):
            return layer * (ITERS + (1 if j == 0 else 0))

        def acc_at(layer, g):
            return SETS + 1 + layer * NG + g

        def rounds(eng, layer, body, setup):
            if layer == 0:
                with eng.Fori(0, EARLY) as i:
                    body(i)
                setup()
                with eng.Fori(EARLY, ITERS) as i:
                    body(i)
                    advance(eng, i)
            else:
                with eng.Fori(0, ITERS) as i:
                    body(i)
                    advance(eng, i)

        steppers = {}
        layer_now = [0]

        def quads_of(eng, name, step):
            reg = eng.alloc_register(name + "_quads")
            steppers[eng] = reg, lambda q, g, n=QB: step(layer_now[0], q, g, n)

        def reset_quads(eng, layer):
            layer_now[0] = layer
            eng.reg_mov(steppers[eng][0], 0)

        def advance(eng, i):
            reg, step = steppers[eng]
            ready = eng.value_load(ready_i[0:1, bass.ds(i * SETS + SETS, 1)], min_val=0, max_val=QUADS - 1)
            done = eng.snap(reg, min_val=0, max_val=QUADS - 1)
            with eng.If(ready > done):
                step(eng.snap(reg, min_val=0, max_val=QUADS - 2), i * SETS + SETS)
                eng.reg_add(reg, reg, 1)

        def finish_quads(eng):
            reg, step = steppers[eng]
            first = eng.snap(reg, min_val=0, max_val=QUADS - 1)
            with eng.If(first < QUADS - 1):
                with eng.Fori(first, QUADS - 1) as q:
                    step(q, None)
            step(QUADS - 1, None, QB_LAST)

        def blocks(bank, n):
            return bank[:, 0:n * P].rearrange("p (x b) -> p x b", x=n)

        def rows_of(dram, q, n):
            return dram[bass.ds(q * QR, n * P), :].rearrange("(b p) d -> p b d", p=P)

        STAGES = LQ + 2
        SELECT_SLOT = 8
        AHEAD = 5
        HELD = 5
        DVE_HELD = 2
        assert 2 * SELECT_SLOT >= STAGES and SELECT_SLOT < LQ

        def stages_of(t):
            return range(2 * t, min(2 * t + 2, STAGES))

        def tiles_beside(k):
            first, end = (AHEAD + (TILES - HELD - AHEAD) * x // STAGES for x in (k, k + 1))
            return range(first, end)

        def tiles_ahead(t):
            last_slots = LQ - 1 - SELECT_SLOT
            first, end = (AHEAD * max(0, x - SELECT_SLOT - 1) // last_slots for x in (t, t + 1))
            return range(first, end)

        held = range(TILES - HELD, TILES)

        def by_dve(b, m):
            return m % 2 == 1 if b == LAST else m in held[1:1 + DVE_HELD]

        def tile_copied(b, m):
            dve = by_dve(b, m)
            earlier = [(x, y) for x in range(b + 1) for y in (range(TILES) if x < b else range(m + 1))]
            return s_copied[dve], sum(by_dve(x, y) == dve for x, y in earlier)

        @block.sync
        def _(sp):
            def edges(src, dst, g0, g1, s):
                sp.dma_start(dst[:, g0 * Q:g1 * Q].rearrange("p (g q) -> p g q", q=Q),
                             src[g0 * GE:g1 * GE].rearrange("(g p q) -> p g q", p=P, q=Q)).then_inc(s, 16)

            def short_group(src, dst, s):
                sp.dma_start(dst[0:TP, FULL * Q:FULL * Q + TQ],
                             src[FULL * GE:NNZ].rearrange("(p q) -> p q", q=TQ)).then_inc(s, 16)

            first = adj_row[0:FULL * GE].rearrange("(g n) -> g n", n=GE)
            edges(adj_col, col, 0, EG, loaded["cols0"])
            sp.dma_start(first_i[0:1, 0:FULL], first[:, 0:1].rearrange("g o -> o g"),
                         allow_slow_non_contiguous=True).then_inc(loaded["first"], 16)
            sp.dma_start(first_i[0:1, FULL:NG], adj_row[FULL * GE:FULL * GE + 1].rearrange("(o n) -> o n", o=1)
                         ).then_inc(loaded["first"], 16)
            edges(adj_row, row_i, 0, EG, loaded["rows0"])
            edges(adj_val, val, 0, EG, loaded["vals0"])
            sp.wait_ge(tail_clear, 1)
            for src, dst, k in ((adj_row, row_i, "rows"), (adj_col, col, "cols"), (adj_val, val, "vals")):
                short_group(src, dst, loaded[k])
            sp.dma_start(last_i[0:1, 0:FULL], first[:, GE - 1:GE].rearrange("g o -> o g"),
                         allow_slow_non_contiguous=True).then_inc(loaded["last"], 16)
            sp.dma_start(last_i[0:1, FULL:NG], adj_row[NNZ - 1:NNZ].rearrange("(o n) -> o n", o=1)
                         ).then_inc(loaded["last"], 16)
            sp.dma_start(w1_sb[:, :, :], w1.rearrange("(h p) e -> p h e", p=P)).then_inc(loaded["weights"], 16)
            sp.dma_start(pos_sb, pos_emb).then_inc(loaded["weights"], 16)
            sp.dma_start(glu_sb[:, 0, :], glu1_w).then_inc(loaded["weights"], 16)
            sp.dma_start(glu_sb[:, 1, :], glu2_w).then_inc(loaded["weights"], 16)
            sp.dma_start(b1[:, :], glu1_b.rearrange("(p o) -> p o", o=1)).then_inc(loaded["weights"], 16)
            sp.dma_start(w2_sb[:, :], w2).then_inc(loaded["weights"], 16)
            for dst, src in ((item_i, items), (inp_i, inputs), (ali_i, alias)):
                sp.dma_start(dst, src.rearrange("(b p) l -> p b l", p=P)).then_inc(loaded["sess"], 16)
            sp.dma_start(gnat_b[0:LASTB, FB, :], E[FB * P:N, :]).then_inc(loaded["E"], 16)
            for n in range(PIECES):
                sp.wait_ge(acc_done, acc_at(0, n * SETS + 1))
                g0, g1 = (EG + (FULL - EG) * x // PIECES for x in (n, n + 1))
                for src, dst, k in ((adj_row, row_i, "rows"), (adj_col, col, "cols"), (adj_val, val, "vals")):
                    edges(src, dst, g0, g1, loaded[k])
                block0, block1 = (FB * x // PIECES for x in (n, n + 1))
                sp.dma_start(gnat_b[:, block0:block1, :], E[block0 * P:block1 * P, :].rearrange("(b p) d -> p b d", p=P)
                             ).then_inc(loaded["E"], 16)

            def store_quad(layer, q, g, n):
                if layer == 0:
                    sp.wait_ge(n_h, q + 1)
                    sp.dma_start(rows_of(h1_dram, q, n), hrow[:, 0:n, :]).then_inc(h_stored, 16)
                else:
                    sp.wait_ge(n_add, q + (QUADS + 1))
                    sp.dma_start(rows_of(gm_dram, q, n)[:, :, 0:D], hrow[:, 0:n, :]).then_inc(g_stored, 16)
                    sp.wait_ge(q_mrow, q + 1)
                    sp.dma_start(rows_of(gm_dram, q, n)[:, :, D:2 * D], mrow[:, 0:n, :]).then_inc(m_stored, 16)

            quads_of(sp, "sp", store_quad)
            sp.wait_ge(tables_ready, 1)
            for layer in range(LAYERS):
                reset_quads(sp, layer)
                with sp.Fori(0 if layer else EARLY, ITERS) as i:
                    advance(sp, i)
                finish_quads(sp)

            def store(b, first, end, src, done):
                n = min(end * ST, N) - first * ST
                for m in range(first, end):
                    sp.wait_ge(*tile_copied(b, m))
                sp.dma_start(scores[b * P:(b + 1) * P, first * ST:first * ST + n], src[:, 0:n]).then_inc(done, 16)

            for b in range(NBATCH):
                for m in range(STORES):
                    first, end = m * TPS, min((m + 1) * TPS, TILES)
                    h = (b * STORES + m) % NSTAGE
                    if b < LAST:
                        store(b, first, end, stages[:, h * SW:(h + 1) * SW], s_out[h])
                    else:
                        store(b, first, end, arena[:, first * ST:], s_out_last)
            for h in range(NSTAGE):
                sp.wait_ge(s_out[h], 16 * len(range(h, LAST * STORES, NSTAGE)))
            sp.wait_ge(s_out_last, 16 * STORES)

        @block.gpsimd
        def _(pool):
            def gather(dst, src, index, s):
                nc.gpsimd.indirect_dma_start(dst, None, src, bass.IndirectOffsetOnAxis(ap=index, axis=0)
                                             ).then_inc(s, 16)

            def gather_group(table, j, use, parts=P, columns=Q):
                pool.wait_ge(idx_ready[j], use + 1)
                pool.sem_inc(pool_go, 1)
                for k in range(columns):
                    gather(gath[0:parts, j * Q + k, :], table, idx_ring[0:parts, j, k:k + 1], landed[j * Q + k])

            slow_groups = pool.alloc_register("pool_slow_groups")
            pool.reg_mov(slow_groups, 0)

            def slow_gathers(table):
                most = pool.value_load(nmax_i[0:1, 0:1], min_val=0, max_val=NB)
                with pool.If(most > 0):
                    with pool.Fori(0, NG) as g:
                        windows = pool.value_load(nwin_i[0:1, bass.ds(g, 1)], min_val=0, max_val=NB)
                        with pool.If(windows > 0):
                            m = pool.snap(slow_groups, min_val=0, max_val=2 * NG)
                            pool.wait_ge(sl_group, m + 1)
                            nc.gpsimd.tensor_copy(idx_ring[:, 0, :], col[:, bass.ds(g * Q, Q)]).then_inc(sl_idx, 1)
                            pool.wait_ge(sl_idx, m + 1)
                            pool.sem_inc(pool_go, 1)
                            for k in range(Q):
                                gather(gath[:, k, :], table, idx_ring[:, 0, k:k + 1], sl_landed[k])
                            pool.reg_add(slow_groups, slow_groups, 1)

            nc.gpsimd.iota(iota_i, pattern=[[1, P]], base=0, channel_multiplier=0).then_inc(pool_const, 1)
            nc.gpsimd.memset(ident[:, :], 0.0).then_inc(pool_const, 1)
            pool.wait_ge(pool_const, 2)
            nc.gpsimd.affine_select(out=ident[:, :], in_=ident[:, :], compare_op=ALU.not_equal, fill=1.0,
                                    base=0, pattern=[[-1, P]], channel_multiplier=1).then_inc(pool_const, 1)

            for layer, table in enumerate((E, h1_dram)):
                if layer:
                    pool.wait_ge(h_stored, 16 * (QUADS + 1))
                with pool.Fori(0, ITERS) as i:
                    for j in range(SETS):
                        gather_group(table, j, used(layer, j) + i)
                gather_group(table, 0, used(layer, 0) + ITERS, TP, TQ)
                pool.wait_ge(tables_ready, 1)
                pool.wait_ge(acc_done, acc_at(layer, NG))
                slow_gathers(table)

            pool.wait_ge(g_stored, 16 * (QUADS + 1))
            pool.wait_ge(m_stored, 16 * (QUADS + 1))
            for b in range(NBATCH):
                h = b % 2
                pool.wait_ge(seq_free[h], b // 2 + 1)
                for l in range(L):
                    gather(seqs[h][:, l, :, :].rearrange("p c d -> p (c d)"), gm_dram, cidx[:, b, l:l + 1],
                           got[h][l // QB])

        def tile_items(m):
            return min(ST, N - m * ST)

        @block.tensor
        def _(pe):
            mm, tr = nc.tensor.matmul, nc.tensor.transpose

            def sum_group(layer, j, use, added, parts=P, columns=Q):
                pe.wait_ge(sel_ready[j], Q * (use + 1))
                pe.wait_ge(acc_done, added - SETS + 1)
                for k in range(columns):
                    s = j * Q + k
                    unused = layer if j == 0 and k >= TQ else 0
                    pe.wait_ge(landed[s], 16 * (use + (1 - unused)))
                    last = mm(win[j][:, 0:W], gath[0:parts, s, :], sel[0:parts, s, :],
                              start=k == 0, stop=k == columns - 1)
                last.then_inc(summed[j], 1)

            slow_groups = pe.alloc_register("pe_slow_groups")
            slow_windows = pe.alloc_register("pe_slow_windows")
            pe.reg_mov(slow_groups, 0)
            pe.reg_mov(slow_windows, 0)

            def slow_sums(layer):
                pe.wait_ge(acc_done, acc_at(layer, NG))
                most = pe.value_load(nmax_i[0:1, 0:1], min_val=0, max_val=NB)
                with pe.If(most > 0):
                    with pe.Fori(0, NG) as g:
                        windows = pe.value_load(nwin_i[0:1, bass.ds(g, 1)], min_val=0, max_val=NB)
                        with pe.If(windows > 0):
                            m = pe.snap(slow_groups, min_val=0, max_val=2 * NG)
                            for k in range(Q):
                                pe.wait_ge(sl_landed[k], 16 * (m + 1))
                            pe.sem_inc(pe_go, 1)
                            with pe.Fori(0, windows):
                                t = pe.snap(slow_windows, min_val=0, max_val=4 * NG)
                                pe.wait_ge(sl_sel, t + 1)
                                for k in range(Q):
                                    last = mm(win[0][:, 0:W], gath[:, k, :], sel[:, k, :], start=k == 0, stop=k == Q - 1)
                                last.then_inc(sl_sum, 1)
                                pe.reg_add(slow_windows, slow_windows, 1)
                            pe.reg_add(slow_groups, slow_groups, 1)

            def quad_products(layer, q, g, n):
                pe.wait_ge(n_cp, q + (layer * QUADS + 1))
                for b in range(n):
                    last = tr(pt[0][:, b * P:(b + 1) * P], quadT[:, b * P:(b + 1) * P], ident[:, :])
                last.then_inc(n_T, 1)
                if layer == LAYERS - 1:
                    pe.wait_ge(n_add, q + (QUADS + 1))
                    for b in range(n):
                        last = tr(pt[1][:, b * P:(b + 1) * P], hrow[:, b, :], ident[:, :])
                    last.then_inc(q_T, 1)
                    pe.wait_ge(q_cp, q + 1)
                    for b in range(n):
                        last = mm(py[1][:, b * D:(b + 1) * D], quadT[:, b * P:(b + 1) * P], w1_sb[:, 1, :],
                                  start=True, stop=True)
                    last.then_inc(q_m, 1)
                    pe.wait_ge(q_g, q + 1)
                    for b in range(n):
                        last = tr(pt[1][:, b * P:(b + 1) * P], grow[:, b, :], ident[:, :])
                    last.then_inc(q_gT, 1)

            def weights():
                pe.wait_ge(pool_const, 3)
                pe.wait_ge(loaded["weights"], 16 * 6)
                tr(pt[1][:, 0:L], pos_sb, ident[0:L, 0:L])
                for w in range(2):
                    last = tr(pt[1][:, (w + 1) * P:(w + 2) * P], glu_sb[:, w, :], ident[:, :])
                last.then_inc(wt_ps, 1)
                pe.wait_ge(wt_sb, 1)
                mm(pt[1][:, 3 * P:3 * P + L], w1_sb[:, 0, :], posT[:, :], start=True, stop=True).then_inc(wt_ps, 1)
                pe.wait_ge(tables_ready, 1)

            pe.wait_ge(first_ready, 1)
            mm(first_bc, ones[:, :], first_f, start=True, stop=True).then_inc(first_ps, 1)
            quads_of(pe, "pe", quad_products)
            for layer in range(LAYERS):
                reset_quads(pe, layer)

                def sums(i):
                    for j in range(SETS):
                        sum_group(layer, j, used(layer, j) + i, i * SETS + (acc_at(layer, 0) + j))

                rounds(pe, layer, sums, weights)
                sum_group(layer, 0, used(layer, 0) + ITERS, acc_at(layer, FULL), TP, TQ)
                slow_sums(layer)
                finish_quads(pe)

            def batch_quad(b, t):
                c = b * LQ + t
                pe.wait_ge(got[b % 2][t], 16 * len(positions(t)) * (b // 2 + 1))
                if c >= 2:
                    pe.wait_ge(s_nh, c - 1)
                for x, l in enumerate(positions(t)):
                    last = tr(pt[c % 2][:, x * P:(x + 1) * P], seqs[b % 2][:, l, 1, :], ident[:, :])
                last.then_inc(s_T, 1)

            def glu_quad(b, t):
                c = b * LQ + t
                n = len(positions(t))
                pe.wait_ge(s_nh, c + 1)
                if c >= 2:
                    pe.wait_ge(s_u, c - 1)
                mm(blocks(py[c % 2], n), gluT[:, 0, :], seqs[b % 2][:, t * QB:t * QB + n, 1, :],
                   start=True, stop=True).then_inc(s_z, 1)

            def beta_quad(b, t):
                c = b * LQ + t
                pe.wait_ge(s_sig, c + 1)
                if t >= 2:
                    pe.wait_ge(s_beta_read, c - 1)
                for l in positions(t):
                    last = mm(beta_banks[t % 2][:, l:l + 1], seqs[b % 2][:, l, 1, :], w2_sb[:, :],
                              start=True, stop=True)
                last.then_inc(s_beta, 1)

            def mean_part(b):
                pe.wait_ge(s_hs, b + 1)
                tr(pm[:, 0:P], hsn[:, :], ident[:, :]).then_inc(s_hsT, 1)
                pe.wait_ge(s_hsc, b + 1)
                mm(pm[:, P:2 * P], gluT[:, 1, :], hsT[:, :], start=True, stop=True).then_inc(s_gp, 1)

            def select_T(b):
                pe.wait_ge(s_sel, b + 1)
                tr(pm[:, 3 * P:4 * P], selrow[:, :], ident[:, :]).then_inc(s_selT, 1)

            def score_tile(b, m):
                n = tile_items(m)
                banks = tile_banks[b]
                pe.wait_ge(s_selc, b + 1)
                if m >= len(banks):
                    pe.wait_ge(*tile_copied(b, m - len(banks)))
                elif b:
                    pe.wait_ge(*tile_copied(b - 1, TILES - 1))
                out = banks[m % len(banks)][:, 0:n]
                mm(out, selT[:, 0, :], split[:, m, 0, 0:n], start=True, stop=False)
                mm(out, selT[:, 0, :], split[:, m, 1, 0:n], start=False, stop=False)
                mm(out, selT[:, 1, :], split[:, m, 0, 0:n], start=False, stop=True).then_inc(s_tile, 1)

            pe.wait_ge(quad_done, 2 * QUADS + 1)
            for b in range(-1, NBATCH):
                for t in range(LQ):
                    if b >= 0:
                        for k in stages_of(t):
                            if k == 0:
                                mean_part(b)
                            if 1 <= k < LQ + 1:
                                beta_quad(b, k - 1)
                            if k + 2 < LQ:
                                glu_quad(b, k + 2)
                            if b:
                                for m in tiles_beside(k):
                                    score_tile(b - 1, m)
                        if t == SELECT_SLOT:
                            if b:
                                for m in held:
                                    score_tile(b - 1, m)
                            select_T(b)
                    if b + 1 < NBATCH:
                        if b >= 0:
                            for m in tiles_ahead(t):
                                score_tile(b, m)
                        if t == LQ - 1:
                            for k in range(2):
                                glu_quad(b + 1, k)
                        batch_quad(b + 1, t)
            for m in range(TILES):
                score_tile(LAST, m)

        def copy_tile(eng, scale, b, m):
            eng.wait_ge(s_tile, b * TILES + m + 1)
            n = b * STORES + m // TPS
            if b == LAST:
                out = arena[:, m * ST:m * ST + tile_items(m)]
            else:
                if n >= NSTAGE:
                    eng.wait_ge(s_out[n % NSTAGE], 16 * (n // NSTAGE))
                at = (n % NSTAGE) * SW + (m % TPS) * ST
                out = stages[:, at:at + tile_items(m)]
            bank = tile_banks[b][m % len(tile_banks[b])]
            scale(out, bank[:, 0:tile_items(m)], 1.0 / (ITEM_SCALE * SELECT_SCALE)).then_inc(tile_copied(b, m)[0], 1)

        @block.scalar
        def _(act):
            def columns(j, use, g):
                act.wait_ge(summed[j], use + 1)
                nc.scalar.copy(idx_ring[:, j, :], col[:, bass.ds(g * Q, Q)]).then_inc(idx_ready[j], 1)

            def quad_norms(layer, q, g, n):
                v = q + layer * QUADS

                def norms(src, which, squared, root):
                    for b in range(n):
                        last = nc.scalar.activation(py[0][:, b * D:(b + 1) * D], src(b), ACT.Square,
                                                    accum_out=ss[:, which, b:b + 1])
                    last.then_inc(squared[0], 1)
                    act.wait_ge(squared[0], squared[1])
                    nc.scalar.activation(nrm[:, which, 0:n], ss[:, which, 0:n], ACT.Sqrt).then_inc(root, 1)

                if g is None:
                    act.wait_ge(acc_complete, layer + 1)
                else:
                    act.wait_ge(acc_done, g + acc_at(layer, 0))
                act.wait_ge(quad_done, v + 1)
                nc.scalar.copy(quadT[:, 0:n * P], accT[:, bass.ds(q * QR, n * P)]).then_inc(n_cp, 1)
                act.wait_ge(n_T, v + 1)
                norms(lambda b: pt[0][:, b * D:(b + 1) * D], 0, (n_ss, v + 1), n_root)
                if layer == LAYERS - 1:
                    act.wait_ge(q_T, q + 1)
                    nc.scalar.copy(quadT[:, 0:n * P], pt[1][:, 0:n * P]).then_inc(q_cp, 1)
                    act.wait_ge(n_add, v + 1)
                    norms(lambda b: hrow[:, b, :], 1, (q_ss, q + 1), q_root)

            quads_of(act, "act", quad_norms)
            nc.scalar.preload_act_table_set("sqrt_and_others")
            act.wait_ge(loaded["cols0"], 16)
            for layer in range(LAYERS):
                reset_quads(act, layer)

                def all_columns(i):
                    for j in range(SETS):
                        columns(j, used(layer, j) + i, i * SETS + j)

                start = 0
                all_columns(0)
                if layer == 0:
                    act.wait_ge(tail_clear, 1)
                    nc.scalar.copy(accT[:, :], zero[:, :].broadcast_to([P, NPAD])).then_inc(acc_done, 1)
                    with act.Fori(0, EARLY - 1) as i:
                        all_columns(i + 1)
                    act.wait_ge(loaded["cols"], 16 * (PIECES + 1))
                    all_columns(EARLY)
                    act.wait_ge(tables_ready, 1)
                    start = EARLY
                with act.Fori(start, ITERS - 1) as i:
                    all_columns(i + 1)
                    advance(act, i)
                columns(0, used(layer, 0) + ITERS, FULL)
                advance(act, ITERS - 1)
                finish_quads(act)

            def tanh_quad(b, t):
                c = b * LQ + t
                act.wait_ge(s_T, c + 1)
                for x, l in enumerate(positions(t)):
                    last = nc.scalar.activation(seqs[b % 2][:, l, 1, :], pt[c % 2][:, x * P:(x + 1) * P],
                                                ACT.Tanh, bias=pw[:, L - 1 - l:L - l])
                last.then_inc(s_nh, 1)

            def sigmoid_quad(b, t):
                quad = seqs[b % 2][:, t * QB:t * QB + len(positions(t)), 1, :]
                act.wait_ge(s_u, b * LQ + t + 1)
                nc.scalar.activation(quad, quad, ACT.Sigmoid).then_inc(s_sig, 1)

            def select_norm(b):
                if b < LAST:
                    nc.scalar.preload_act_table_set("sqrt_and_others")
                act.wait_ge(s_sess, b + 1)
                nc.scalar.activation(selrow[:, :], sess[:, :], ACT.Square, accum_out=sn[:, 0:1]).then_inc(s_sq, 1)
                act.wait_ge(s_sq, 2 * b + 1)
                nc.scalar.activation(sn[:, 1:2], sn[:, 0:1], ACT.Sqrt).then_inc(s_sq, 1)

            act.wait_ge(quad_done, 2 * QUADS + 1)
            nc.scalar.preload_act_table_set("sigmoid_and_others")
            for b in range(-1, NBATCH):
                for t in range(LQ):
                    if b >= 0:
                        for k in stages_of(t):
                            if k < LQ:
                                sigmoid_quad(b, k)
                            if b == LAST and k == LQ:
                                nc.scalar.preload_act_table_set("sqrt_and_others")
                            if b:
                                for m in tiles_beside(k):
                                    copy_tile(act, nc.scalar.mul, b - 1, m)
                        if t == SELECT_SLOT:
                            if b:
                                copy_tile(act, nc.scalar.mul, b - 1, held[0])
                            select_norm(b)
                            if b:
                                for m in held[1 + DVE_HELD:]:
                                    copy_tile(act, nc.scalar.mul, b - 1, m)
                            if b + 1 < NBATCH:
                                nc.scalar.preload_act_table_set("sigmoid_and_others")
                    if b + 1 < NBATCH:
                        if b >= 0:
                            for m in tiles_ahead(t):
                                copy_tile(act, nc.scalar.mul, b, m)
                        tanh_quad(b + 1, t)
            for m in range(0, TILES, 2):
                copy_tile(act, nc.scalar.mul, LAST, m)

        @block.vector
        def _(dve):
            v = nc.vector
            steps = [0]

            def mark(ins):
                steps[0] += 1
                ins.then_inc(vchain, 1)

            def link(ins):
                mark(ins)
                dve.wait_ge(vchain, steps[0])

            mark(v.memset(col[:, FULL * Q:NG * Q], 0))
            mark(v.memset(val[:, FULL * Q:NG * Q], 0.0))
            mark(v.memset(rowrel[:, FULL * Q:NG * Q], -1.0))
            mark(v.memset(ones[:, :], 1.0))
            mark(v.memset(zero[:, :], 0.0))
            link(v.memset(gnat_b[:, FB:NB, :], 0.0))
            dve.sem_inc(tail_clear, 1)
            for j in range(SETS):
                dve.sem_inc(summed[j], 1)
            dve.sem_inc(acc_done, SETS)
            for s in (sl_group, quad_done, seq_free[0], seq_free[1]):
                dve.sem_inc(s, 1)
            for s in (h_stored, g_stored, m_stored):
                dve.sem_inc(s, 16)
            dve.wait_ge(pool_const, 1)
            mark(v.tensor_copy(iota[:, :], iota_i))
            dve.wait_ge(loaded["first"], 32)
            link(v.tensor_copy(first_f, first_i[:, :]))
            dve.sem_inc(first_ready, 1)

            def relative_rows(g0, g1):
                mark(v.tensor_tensor(rowrel[:, g0 * Q:g1 * Q].rearrange("p (g q) -> p g q", q=Q),
                                     row_i[:, g0 * Q:g1 * Q].rearrange("p (g q) -> p g q", q=Q),
                                     first_bc[:, g0:g1].unsqueeze(2).broadcast_to([P, g1 - g0, Q]), ALU.subtract))

            dve.wait_ge(first_ps, 1)
            dve.wait_ge(loaded["rows0"], 16)
            relative_rows(0, EG)
            dve.wait_ge(vchain, steps[0])
            dve.wait_ge(loaded["vals0"], 16)

            def late():
                dve.wait_ge(loaded["rows"], 16 * (PIECES + 1))
                relative_rows(EG, FULL)
                tail = slice(FULL * Q, FULL * Q + TQ)
                link(v.tensor_tensor(rowrel[0:TP, tail], row_i[0:TP, tail],
                                     first_bc[0:TP, FULL:NG].broadcast_to([TP, TQ]), ALU.subtract))
                dve.wait_ge(loaded["last"], 32)
                link(v.tensor_tensor(span_i, last_i, first_i[:, :], ALU.subtract))
                link(v.tensor_scalar(nwin_i[:, :], span_i, W.bit_length() - 1, None, ALU.arith_shift_right))
                link(v.tensor_reduce(nmax_i[:, :], nwin_i[:, :], AX.X, ALU.max))
                mark(v.tensor_scalar(ok_f, nmax_i[:, :], 0.0, None, ALU.is_equal))
                link(v.tensor_scalar(span_i, first_i[:, :], QR.bit_length() - 1, None, ALU.arith_shift_right))
                link(v.tensor_scalar(ready_i[:, :], span_i, ok_f, None, ALU.mult))
                dve.sem_inc(tables_ready, 1)
                dve.wait_ge(loaded["vals"], 16 * (PIECES + 1))

            def weights_and_sessions():
                dve.wait_ge(wt_ps, 1)
                mark(v.tensor_copy(posT[:, :], pt[1][:, 0:L]))
                link(v.tensor_copy(gluT[:, :, :], pt[1][:, P:3 * P].rearrange("p (w f) -> p w f", w=2)))
                dve.sem_inc(wt_sb, 1)
                dve.wait_ge(wt_ps, 2)
                link(v.tensor_copy(pw[:, :], pt[1][:, 3 * P:3 * P + L]))
                dve.wait_ge(loaded["sess"], 48)
                mark(v.memset(cidx_f, 0.0))
                mark(v.tensor_copy(item_f, item_i))
                mark(v.tensor_copy(ali_f, ali_i))
                link(v.tensor_scalar(mask[:, :, :], inp_i, 0.0, None, ALU.not_equal))
                mark(v.tensor_reduce(cnt[:, :], mask[:, :, :], AX.X, ALU.add))
                link(v.tensor_scalar(pick, item_f, 0.0, float(N), ALU.is_lt, ALU.mult))
                mark(v.reciprocal(rcnt[:, :], cnt[:, :]))
                link(v.tensor_tensor(item_f, item_f, pick, ALU.add))
                link(v.tensor_scalar(item_f, item_f, 0.0, float(N - 1), ALU.max, ALU.min))

            def select_group(j, use, g):
                dve.wait_ge(summed[j], use + 1)
                for k in range(Q):
                    v.tensor_scalar(sel[:, j * Q + k, :], iota[:, :], rowrel[:, bass.ds(g * Q + k, 1)],
                                    val[:, bass.ds(g * Q + k, 1)], ALU.is_equal, ALU.mult).then_inc(sel_ready[j], 1)

            def add_group(layer, j, use, g):
                row0 = dve.value_load(first_i[0:1, bass.ds(g, 1)], min_val=0, max_val=N - 1)
                dve.wait_ge(summed[j], use + 2)
                dve.wait_ge(acc_done, acc_at(layer, 0) + g)
                dst = accT[:, bass.ds(row0, W)]
                v.tensor_tensor(dst, dst, win[j][:, 0:W], ALU.add).then_inc(acc_done, 1)

            def adds(layer, i):
                for j in range(SETS):
                    nj, more = (j + 1) % SETS, (j + 1) // SETS
                    select_group(nj, used(layer, nj) + i + more, i * SETS + j + 1)
                    add_group(layer, j, used(layer, j) + i, i * SETS + j)

            slow_windows = dve.alloc_register("dve_slow_windows")
            dve.reg_mov(slow_windows, 0)
            place = dve.alloc_register("dve_window_row")

            def slow_adds():
                most = dve.value_load(nmax_i[0:1, 0:1], min_val=0, max_val=NB)
                with dve.If(most > 0):
                    with dve.Fori(0, NG) as g:
                        windows = dve.value_load(nwin_i[0:1, bass.ds(g, 1)], min_val=0, max_val=NB)
                        with dve.If(windows > 0):
                            row0 = dve.value_load(first_i[0:1, bass.ds(g, 1)], min_val=0, max_val=N - 1)
                            v.tensor_copy(rowm[:, :], rowrel[:, bass.ds(g * Q, Q)])
                            dve.drain()
                            dve.reg_mov(place, row0)
                            with dve.Fori(0, windows):
                                v.tensor_scalar(rowm[:, :], rowm[:, :], float(W), None, ALU.subtract)
                                dve.drain()
                                for k in range(Q):
                                    v.tensor_scalar(sel[:, k, :], iota[:, :], rowm[:, k:k + 1],
                                                    val[:, bass.ds(g * Q + k, 1)], ALU.is_equal, ALU.mult)
                                dve.drain()
                                dve.sem_inc(sl_sel, 1)
                                t = dve.snap(slow_windows, min_val=0, max_val=4 * NG)
                                dve.wait_ge(sl_sum, t + 1)
                                dve.reg_add(place, place, W)
                                dst = accT[:, bass.ds(dve.snap(place, min_val=W, max_val=N - 1), W)]
                                v.tensor_tensor(dst, dst, win[0][:, 0:W], ALU.add)
                                dve.drain()
                                dve.reg_add(slow_windows, slow_windows, 1)
                            dve.sem_inc(sl_group, 1)

            def over(x, n):
                return x.unsqueeze(2).broadcast_to([P, n, D])

            def quad_rows(layer, q, g, n):
                w = q + layer * QUADS
                parts_of_mean = 1.0 if layer < LAYERS - 1 else float(LAYERS + 1)
                dve.wait_ge(n_cp, w + 1)
                if layer < LAYERS - 1:
                    v.tensor_copy(accT[:, bass.ds(q * QR, n * P)], zero[:, :].broadcast_to([P, n * P])).then_inc(n_clear, 1)
                    dve.wait_ge(n_clear, w + 1)
                dve.wait_ge(n_root, w + 1)
                v.tensor_scalar(nmx[:, 0, 0:n], nrm[:, 0, 0:n], EPS, parts_of_mean, ALU.max, ALU.mult).then_inc(n_rn, 1)
                dve.wait_ge(n_rn, w * 2 + 1)
                v.reciprocal(rn[:, 0, 0:n], nmx[:, 0, 0:n]).then_inc(n_rn, 1)
                dve.wait_ge(n_rn, w * 2 + 2)
                stored = (h_stored, g_stored)[layer]
                dve.wait_ge(stored, q * 16 + 16)
                v.tensor_tensor(hrow[:, 0:n, :], blocks(pt[0], n), over(rn[:, 0, 0:n], n), ALU.mult
                                ).then_inc(n_h, 1)
                dve.wait_ge(n_h, w + 1)
                here = gnat_b[:, bass.ds(q * QB, n), :]
                total = here if layer < LAYERS - 1 else hrow[:, 0:n, :]
                v.scalar_tensor_tensor(total, here, 1.0 / parts_of_mean, hrow[:, 0:n, :], ALU.mult, ALU.add).then_inc(n_add, 1)
                dve.wait_ge(n_add, w + 1)
                if layer == LAYERS - 1:
                    dve.wait_ge(q_m, q + 1)
                    dve.wait_ge(m_stored, q * 16 + 16)
                    v.tensor_copy(mrow[:, 0:n, :], blocks(py[1], n)).then_inc(q_mrow, 1)
                    dve.wait_ge(q_root, q + 1)
                    v.tensor_scalar(nmx[:, 1, 0:n], nrm[:, 1, 0:n], EPS, None, ALU.max).then_inc(q_rn, 1)
                    dve.wait_ge(q_rn, q * 2 + 1)
                    v.reciprocal(rn[:, 1, 0:n], nmx[:, 1, 0:n]).then_inc(q_rn, 1)
                    dve.wait_ge(q_rn, q * 2 + 2)
                    v.tensor_tensor(grow[:, 0:n, :], hrow[:, 0:n, :], over(rn[:, 1, 0:n], n), ALU.mult).then_inc(q_g, 1)
                    dve.wait_ge(q_gT, q + 1)
                    high, low = (accT[:, bass.ds(q * QR + x * (QR // 2), n * P // 2)].bitcast(F16) for x in range(2))
                    v.tensor_scalar(high, pt[1][:, 0:n * P], ITEM_SCALE, None, ALU.mult).then_inc(q_split, 1)
                    dve.wait_ge(q_split, q * 2 + 1)
                    v.scalar_tensor_tensor(low, pt[1][:, 0:n * P], ITEM_SCALE, high, ALU.mult, ALU.subtract
                                           ).then_inc(q_split, 1)
                    dve.wait_ge(q_split, q * 2 + 2)
                    dve.wait_ge(q_mrow, q + 1)
                dve.sem_inc(quad_done, 1)

            quads_of(dve, "dve", quad_rows)
            for layer in range(LAYERS):
                reset_quads(dve, layer)

                select_group(0, used(layer, 0), 0)
                if layer == 0:
                    with dve.Fori(0, EARLY) as i:
                        adds(layer, i)
                    late()
                    weights_and_sessions()
                    dve.wait_ge(loaded["E"], 16 * (PIECES + 1))
                    c0 = steps[0]
                    with dve.Fori(EARLY, EARLY + L) as i:
                        adds(layer, i)
                        here = item_f[:, :, bass.ds(i - EARLY, 1)].broadcast_to([P, NBATCH, L])
                        v.scalar_tensor_tensor(pick, ali_f, 0.0, here, ALU.is_equal, ALU.mult).then_inc(vchain, 1)
                        dve.wait_ge(vchain, i * 3 + (c0 + 1 - 3 * EARLY))
                        v.tensor_tensor(cidx_f, cidx_f, pick, ALU.add).then_inc(vchain, 1)
                        v.tensor_scalar(ali_f, ali_f, -1.0, None, ALU.add).then_inc(vchain, 1)
                        dve.wait_ge(vchain, i * 3 + (c0 + 3 - 3 * EARLY))
                        advance(dve, i)
                    steps[0] += 3 * L
                    link(v.tensor_copy(cidx[:, :, :], cidx_f))
                    with dve.Fori(EARLY + L, ITERS) as i:
                        adds(layer, i)
                        advance(dve, i)
                else:
                    with dve.Fori(0, ITERS) as i:
                        adds(layer, i)
                        advance(dve, i)
                add_group(layer, 0, used(layer, 0) + ITERS, FULL)
                dve.wait_ge(acc_done, acc_at(layer, NG))
                slow_adds()
                dve.drain()
                dve.sem_inc(acc_complete, 1)
                finish_quads(dve)

            def session_sum(part, b, t, weight_of):
                for l in positions(t):
                    row, dst = seqs[b % 2][:, l, 0, :], part[:, l % 2, :]
                    if l >= 2:
                        dve.wait_ge(vchain, steps[0] - 1)
                        mark(v.scalar_tensor_tensor(dst, row, weight_of(l), dst, ALU.mult, ALU.add))
                    else:
                        mark(v.tensor_scalar(dst, row, weight_of(l), None, ALU.mult))

            def mean_quad(b, t):
                dve.wait_ge(got[b % 2][t], 16 * len(positions(t)) * (b // 2 + 1))
                session_sum(hs_part, b, t, lambda l: mask[:, b, l:l + 1])

            def mean_part(b):
                dve.wait_ge(vchain, steps[0])
                link(v.tensor_tensor(hsn[:, :], hs_part[:, 0, :], hs_part[:, 1, :], ALU.add))
                v.tensor_scalar(hsn[:, :], hsn[:, :], rcnt[:, b:b + 1], None, ALU.mult).then_inc(s_hs, 1)
                dve.wait_ge(s_hsT, b + 1)
                v.tensor_copy(hsT[:, :], pm[:, 0:P]).then_inc(s_hsc, 1)
                dve.wait_ge(s_gp, b + 1)
                link(v.tensor_scalar(gb[:, :], pm[:, P:2 * P], b1[:, 0:1], None, ALU.add))

            def add_mean(b, t):
                c, n = b * LQ + t, len(positions(t))
                dve.wait_ge(s_z, c + 1)
                v.tensor_tensor(seqs[b % 2][:, t * QB:t * QB + n, 1, :], blocks(py[c % 2], n),
                                gb[:, :].unsqueeze(1).broadcast_to([P, n, P]), ALU.add).then_inc(s_u, 1)

            def scale(out, x, factor):
                return v.tensor_scalar(out, x, factor, None, ALU.mult)

            def attend(b, t):
                first, end = positions(t)[0], positions(t)[-1] + 1
                dve.wait_ge(s_beta, b * LQ + t + 1)
                v.tensor_tensor(beta[:, first:end], beta_banks[t % 2][:, first:end], mask[:, b, first:end], ALU.mult
                                ).then_inc(s_beta_read, 1)
                dve.wait_ge(s_beta_read, b * LQ + t + 1)
                session_sum(sess_part, b, t, lambda l: beta[:, l:l + 1])

            def select(b):
                dve.wait_ge(vchain, steps[0])
                link(v.tensor_tensor(sess[:, :], sess_part[:, 0, :], sess_part[:, 1, :], ALU.add))
                dve.sem_inc(s_sess, 1)
                dve.sem_inc(seq_free[b % 2], 1)
                if b:
                    for m in held[1:1 + DVE_HELD]:
                        copy_tile(dve, scale, b - 1, m)
                dve.wait_ge(s_sq, 2 * b + 2)
                link(v.tensor_scalar(sn[:, 2:3], sn[:, 1:2], EPS, None, ALU.max))
                link(v.reciprocal(sn[:, 3:4], sn[:, 2:3]))
                v.tensor_scalar(selrow[:, :], sess[:, :], sn[:, 3:4], W_K * SELECT_SCALE, ALU.mult, ALU.mult).then_inc(s_sel, 1)
                dve.wait_ge(s_selT, b + 1)
                if b:
                    dve.wait_ge(s_tile, b * TILES)
                link(v.tensor_copy(selT[:, 0, :], pm[:, 3 * P:4 * P]))
                v.tensor_tensor(selT[:, 1, :], pm[:, 3 * P:4 * P], selT[:, 0, :], ALU.subtract).then_inc(s_selc, 1)

            dve.drain()
            for b in range(-1, NBATCH):
                if b >= 0:
                    mean_part(b)
                for t in range(LQ):
                    if b >= 0:
                        for k in stages_of(t):
                            if k < LQ:
                                add_mean(b, k)
                            if k >= 2:
                                attend(b, k - 2)
                        if t == SELECT_SLOT:
                            select(b)
                    if b + 1 < NBATCH:
                        mean_quad(b + 1, t)
            for m in range(1, TILES, 2):
                copy_tile(dve, scale, LAST, m)


_INS = ["r_items", "r_inputs", "r_alias_inputs", "L0_rec_adj_row", "L0_rec_adj_col", "L0_rec_adj_val",
        "L0_rec_E", "L0_rec_pos_emb", "L0_rec_w1", "L0_rec_w2", "L0_rec_glu1_w", "L0_rec_glu1_b", "L0_rec_glu2_w"]


def kernel(**inputs):
    import numpy as np
    import concourse.bacc as bacc
    from concourse.bass_utils import run_bass_kernel_spmd

    nc = bacc.Bacc("TRN2", target_bir_lowering=False, num_devices=1)
    arrays, args = {}, []
    for name in _INS:
        a = np.ascontiguousarray(inputs[name])
        arrays[f"in_{name}"] = a
        args.append(nc.dram_tensor(f"in_{name}", a.shape, mybir.dt.from_np(a.dtype), kind="ExternalInput").ap())
    shape = (inputs["r_items"].shape[0], inputs["L0_rec_E"].shape[0])
    scores = nc.dram_tensor("scores", shape, F32, kind="ExternalOutput").ap()
    session_graph_scores(nc, *args, scores)
    r = run_bass_kernel_spmd(nc, [arrays], core_ids=[0])
    return r.results[0]["scores"]
```
